# Optimizing a Trainium2 kernel written in Bass

```python
import numpy as np
import jax
import jax.numpy as jnp

def _softmax(x, axis=-1):
    return jax.nn.softmax(x, axis=axis)

def _gelu(x):
    return jax.nn.gelu(x, approximate=True)

def _silu(x):
    return jax.nn.silu(x)

def _sigmoid(x):
    return jax.nn.sigmoid(x)

def _layernorm(x, axis=-1, eps=1e-05):
    m = jnp.mean(x, axis=axis, keepdims=True)
    v = jnp.var(x, axis=axis, keepdims=True)
    return (x - m) / jnp.sqrt(v + eps)

def _scatter_add(tgt, idx, src, axis=0):
    return tgt.at[idx].add(src)

def _segment_sum(src, seg, n):
    return jax.ops.segment_sum(src, seg, n)
kernel_name = 'mk_gnn_resnorm_d1_gnn_r8_0c3a28'

def setup_inputs(seed: int=0):
    np.random.seed(seed)
    _w = jnp.asarray

    def _rec_inputs():
        import jax
        import jax.numpy as jnp
        _gk = jax.random.key(seed)
        x = -0.000202 + 1 * jax.random.normal(jax.random.fold_in(_gk, 1), (12500, 128), jnp.float32)
        src = jax.random.randint(jax.random.fold_in(_gk, 2), (200000,), 0, 12500, jnp.int32)
        dst = jnp.minimum((12500 * jax.random.uniform(jax.random.fold_in(_gk, 3), (200000,)) ** 2.0).astype(jnp.int32), 99999)
        _o = jnp.argsort(dst, stable=True)
        src = src[_o]
        dst = dst[_o]
        edge_attr_128 = 7.68618e-05 + 1.00005 * jax.random.normal(jax.random.fold_in(_gk, 11), (200000, 128), jnp.float32)
        return (x, src, dst, edge_attr_128)
    x, src, dst, edge_attr_128 = _rec_inputs()

    def _L0_gnn_setup():
        import jax, jax.numpy as jnp
        import numpy as np
        HIDDEN = 128
        HEADS = 8
        HEAD_DIM = HIDDEN // HEADS
        N_NODES = 6250
        N_EDGES = 62500
        key = jax.random.key(seed)
        ks = jax.random.split(key, 12)
        s = 1.0 / np.sqrt(HIDDEN)
        inp = {'edge_state': jax.random.normal(ks[0], (N_NODES, HIDDEN), jnp.float32), 'lg_edge_index': jax.random.randint(ks[1], (2, N_EDGES), 0, N_NODES, jnp.int64), 'angle_emb': jax.random.normal(ks[2], (N_EDGES, HIDDEN), jnp.float32), 'Wq': jax.random.normal(ks[3], (HIDDEN, HIDDEN), jnp.float32) * s, 'bq': jnp.zeros((HIDDEN,), jnp.float32), 'Wk': jax.random.normal(ks[4], (HIDDEN, HIDDEN), jnp.float32) * s, 'bk': jnp.zeros((HIDDEN,), jnp.float32), 'Wv': jax.random.normal(ks[5], (HIDDEN, HIDDEN), jnp.float32) * s, 'bv': jnp.zeros((HIDDEN,), jnp.float32), 'We': jax.random.normal(ks[6], (HIDDEN, HIDDEN), jnp.float32) * s, 'Wskip': jax.random.normal(ks[7], (HIDDEN, HIDDEN), jnp.float32) * s, 'bskip': jnp.zeros((HIDDEN,), jnp.float32), 'Wbeta': jax.random.normal(ks[8], (3 * HIDDEN, 1), jnp.float32) * s, 'ln_gamma': jnp.ones((HIDDEN,), jnp.float32), 'ln_beta': jnp.zeros((HIDDEN,), jnp.float32)}
        return inp
    _L0_gnn_all = _L0_gnn_setup()
    _L0_gnn_in = {k: v for k, v in _L0_gnn_all.items() if k in ('Wq', 'bq', 'Wk', 'bk', 'Wv', 'bv', 'We', 'Wskip', 'bskip', 'Wbeta', 'ln_gamma', 'ln_beta')}
    del _L0_gnn_all
    return {'x': x, 'src': src, 'dst': dst, 'edge_attr_128': edge_attr_128, 'L0_gnn_Wq': _L0_gnn_in['Wq'], 'L0_gnn_bq': _L0_gnn_in['bq'], 'L0_gnn_Wk': _L0_gnn_in['Wk'], 'L0_gnn_bk': _L0_gnn_in['bk'], 'L0_gnn_Wv': _L0_gnn_in['Wv'], 'L0_gnn_bv': _L0_gnn_in['bv'], 'L0_gnn_We': _L0_gnn_in['We'], 'L0_gnn_Wskip': _L0_gnn_in['Wskip'], 'L0_gnn_bskip': _L0_gnn_in['bskip'], 'L0_gnn_Wbeta': _L0_gnn_in['Wbeta'], 'L0_gnn_ln_gamma': _L0_gnn_in['ln_gamma'], 'L0_gnn_ln_beta': _L0_gnn_in['ln_beta']}

def reference(x, src, dst, edge_attr_128, L0_gnn_Wq, L0_gnn_bq, L0_gnn_Wk, L0_gnn_bk, L0_gnn_Wv, L0_gnn_bv, L0_gnn_We, L0_gnn_Wskip, L0_gnn_bskip, L0_gnn_Wbeta, L0_gnn_ln_gamma, L0_gnn_ln_beta):
    import jax
    import jax.numpy as jnp

    def _L0_gnn_ref(edge_state, lg_edge_index, angle_emb, Wq, bq, Wk, bk, Wv, bv, We, Wskip, bskip, Wbeta, ln_gamma, ln_beta):
        import jax, jax.numpy as jnp
        import numpy as np
        HIDDEN = 128
        HEADS = 8
        HEAD_DIM = HIDDEN // HEADS
        N_NODES = 6250
        N_EDGES = 62500
        N = edge_state.shape[0]
        H, D = (HEADS, HEAD_DIM)
        src = lg_edge_index[0]
        dst = lg_edge_index[1]
        q = (edge_state @ Wq + bq).reshape(N, H, D)
        k = (edge_state @ Wk + bk).reshape(N, H, D)
        v = (edge_state @ Wv + bv).reshape(N, H, D)
        e = (angle_emb @ We).reshape(-1, H, D)
        k_e = k[src] + e
        v_e = v[src] + e
        alpha = jnp.einsum('ehd,ehd->eh', q[dst], k_e) / jnp.sqrt(jnp.float32(D))
        m = jax.ops.segment_max(alpha, dst, num_segments=N)
        a = jnp.exp(alpha - m[dst])
        z = jax.ops.segment_sum(a, dst, num_segments=N)
        attn = a / z[dst]
        out = jax.ops.segment_sum(attn[:, :, None] * v_e, dst, num_segments=N)
        out = out.reshape(N, H * D)
        x_r = edge_state @ Wskip + bskip
        beta = jax.nn.sigmoid(jnp.concatenate([out, x_r, out - x_r], axis=-1) @ Wbeta)
        out = beta * x_r + (1.0 - beta) * out
        mu = jnp.mean(out, axis=-1, keepdims=True)
        var = jnp.mean(jnp.square(out - mu), axis=-1, keepdims=True)
        out = (out - mu) / jnp.sqrt(var + 1e-05) * ln_gamma + ln_beta
        return edge_state + jax.nn.relu(out)
    edge_index = jnp.stack([src, dst])
    x = _layernorm(x + _L0_gnn_ref(x, edge_index, edge_attr_128, L0_gnn_Wq, L0_gnn_bq, L0_gnn_Wk, L0_gnn_bk, L0_gnn_Wv, L0_gnn_bv, L0_gnn_We, L0_gnn_Wskip, L0_gnn_bskip, L0_gnn_Wbeta, L0_gnn_ln_gamma, L0_gnn_ln_beta), axis=-1)
    return x

_drawn_inputs = setup_inputs


def setup_inputs(seed=0):
    import zlib

    import numpy as np

    out = dict(_drawn_inputs(seed))
    spreads = {'L0_gnn_bq': (0.0, 0.386),
     'L0_gnn_bk': (0.0, 0.8),
     'L0_gnn_bv': (0.0, 0.1),
     'L0_gnn_bskip': (0.0, 0.1),
     'L0_gnn_ln_gamma': (1.0, 0.2),
     'L0_gnn_ln_beta': (0.0, 0.1)}
    factors = {}
    for name, (base, spread) in spreads.items():
        noise = np.random.default_rng([zlib.crc32(name.encode()), seed]).standard_normal(out[name].shape)
        drawn = base * np.exp(spread * noise) if base else spread * noise
        out[name] = jnp.asarray(drawn.astype(out[name].dtype))
    for name, factor in factors.items():
        out[name] = (out[name] * factor).astype(out[name].dtype)
    return out
```

```python
from contextlib import ExitStack

import concourse.bass as bass
from concourse import mybir

F32 = mybir.dt.float32
BF16 = mybir.dt.bfloat16
I32 = mybir.dt.int32
ALU = mybir.AluOpType
ACT = mybir.ActivationFunctionType
AX_X = mybir.AxisListType.X
RMAX = bass.bass_isa.ReduceOp.max

P = 128
H = 8
D = 16
C = H * D
N_NODES = 12500
N_EDGES = 200000
TILES_G = 4
EDGES_G = TILES_G * P
TILES_Q = 2 * TILES_G
PAIRS = 2 * -(-N_EDGES // (4 * EDGES_G))
GROUPS = 2 * PAIRS
TILES = GROUPS * TILES_G
EDGES = TILES * P
BLOCKS = 99
ROWS = BLOCKS * P
OUT_BLOCKS = 98
AC = C + H
PAIR = TILES_Q * P
EPS = 1e-5
RANGE = 60.0
BIG = 1e30

TB = 3
TSLOTS = 3
FB = 7
ZERO_DMAS = 11
ZERO_W = BLOCKS * AC // ZERO_DMAS


def build(nc, xT, x, eaT, srcT, dstT, dst, w, out):
    ctx = ExitStack()
    with ctx:
        def sb(name, shape, dt=F32):
            return ctx.enter_context(nc.sbuf_tensor(name, shape, dt))

        def ps(name, shape):
            return ctx.enter_context(nc.psum_tensor(name, shape, F32))

        def sem(name):
            return ctx.enter_context(nc.semaphore(name))

        kv_tab = nc.dram_tensor("kv_tab", (ROWS, 2 * C), F32).ap()
        q_tab = nc.dram_tensor("q_tab", (ROWS, C), F32).ap()
        sum_tab = nc.dram_tensor("sum_tab", (ROWS, AC), F32).ap()
        max_tab = nc.dram_tensor("max_tab", (ROWS, H), F32).ap()
        rel_row = nc.dram_tensor("rel_row", (1, EDGES), BF16).ap()

        e_ps = [ps(f"e_ps{u}", [P, 512]) for u in range(2)]
        q_ps = [ps(f"q_ps{u}", [P, 512]) for u in range(2)]
        sum_ps = [ps(f"sum_ps{u}", [P, 512]) for u in range(2)]
        row_ps = ps("row_ps", [P, 512])
        max_ps = ps("max_ps", [P, 512])

        w_kvq = sb("w_kvq", [P, 3 * C])
        b_kvq = sb("b_kvq", [P, 3 * C])
        we = sb("we", [P, C])
        wskip = sb("wskip", [P, C])
        bskip = sb("bskip", [P, C])
        wbeta = sb("wbeta", [P, 3, C])
        w_out = sb("w_out", [P, C])
        w_skip = sb("w_skip", [P, C])
        gamma = sb("gamma", [P, C])
        beta_ln = sb("beta_ln", [P, C])
        ident = sb("ident", [P, P])
        ones_f = sb("ones_f", [1, P])
        ones_b = sb("ones_b", [1, P], BF16)
        iota_n = sb("iota_n", [P, P])
        iota_pn = sb("iota_pn", [P, P])
        neg_p = sb("neg_p", [P, 1])
        zeros = sb("zeros", [P, ZERO_W])
        one_col = sb("one_col", [P, 1])

        xt_buf = sb("xt_buf", [P, TSLOTS, TB * P])
        tab_buf = sb("tab_buf", [P, TSLOTS, TB, 3 * C])

        src_all = sb("src_all", [P, TILES], I32)
        dst_all = sb("dst_all", [P, TILES], I32)
        neg_rel = sb("neg_rel", [P, TILES])
        first = sb("first", [1, GROUPS])
        first_b = sb("first_b", [P, GROUPS])
        delta = sb("delta", [P, GROUPS])
        rel_rows = sb("rel_rows", [PAIRS // 2, 2 * PAIR], BF16)
        bad = sb("bad", [P, 4])
        bad_all = sb("bad_all", [P, 1])
        flag = sb("flag", [P, 1], I32)
        spread = sb("spread", [P, 4])
        wide = sb("wide", [P, 1], I32)

        idx = sb("idx", [P, 2, TILES_Q], I32)
        kv = sb("kv", [P, 4, TILES_G, 2 * C])
        ea = sb("ea", [P, 2, 2 * EDGES_G])
        row = sb("row", [1, 2, 2 * EDGES_G], BF16)
        q_win = sb("q_win", [P, 4, C])
        dist = sb("dist", [P, 2, EDGES_G], BF16)
        hot_ne = sb("hot_ne", [P, 2, EDGES_G])
        dist_en = sb("dist_en", [P, 2, TILES_G, P], BF16)
        hot_en = sb("hot_en", [P, 4, TILES_G, P])
        kve = sb("kve", [P, 4, TILES_G, 2, C])
        prod = sb("prod", [P, 2, EDGES_G])
        logit = sb("logit", [P, TILES * H])
        top = sb("top", [P, 1])
        neg_pair = sb("neg_pair", [1, 1])
        neg_max = sb("neg_max", [1, 2])
        neg_max_b = sb("neg_max_b", [P, 2])
        fade = sb("fade", [P, 2])
        wv = sb("wv", [P, 4, TILES_G, AC])
        shift = sb("shift", [P, 2, P])
        sums = sb("sums", [P, 4, AC])
        ends = sb("ends", [P, 2])

        g_kve = kve[:, 2, 0, :, :]
        g_kv = kv[:, 0, 0, :]
        g_q = kv[:, 0, 1, 0:C]
        g_ea = ea[:, 0, 0:P]
        g_prod = prod[:, 0, 0:C]
        g_dst = xt_buf[:, 0, 0:P].bitcast(I32)
        g_dst_f = xt_buf[:, 1, 0:P]
        g_same = hot_ne[:, 0, 0:P]
        g_apart = hot_ne[:, 0, P:2 * P]
        g_before = hot_ne[:, 0, 2 * P:3 * P]
        g_own = kve[:, 0, :, :, :].rearrange("p t a c -> p (t a) c")
        g_peers = kve[:, 1, :, :, :].rearrange("p t a c -> p (t a) c")
        g_wv = wv[:, 0, 0, :]
        g_old = sums[:, 0, :]
        g_new = sums[:, 1, :]
        g_low = tab_buf[:, 0, :, :].rearrange("p b c -> p (b c)")[:, 0:BLOCKS * H]
        g_logit = sb("g_logit", [P, H])
        g_old_max = sb("g_old_max", [P, H])
        g_max = sb("g_max", [P, H])
        g_exp = sb("g_exp", [P, 2, H])
        g_node = sb("g_node", [P, 2])
        g_idx = sb("g_idx", [P, 2], I32)
        g_put = sb("g_put", [P, 1], I32)

        dst_rows = logit[0:PAIRS // 2, 0:2 * PAIR].bitcast(I32)
        dst_rows_f = logit[0:PAIRS // 2, 2 * PAIR:4 * PAIR]
        carve = [0]

        def part(*shape):
            size = 1
            for n in shape:
                size *= n
            view = logit[:, carve[0]:carve[0] + size]
            carve[0] += size
            if len(shape) == 1:
                return view
            names = ["a", "b", "c"][:len(shape)]
            return view.rearrange(f"p ({' '.join(names)}) -> p {' '.join(names)}", **dict(zip(names, shape)))

        n_sum = [part(FB, AC) for _ in range(2)]
        n_x = [part(FB, C) for _ in range(2)]
        n_xt = [part(FB * P) for _ in range(2)]
        n_y = [part(FB, C) for _ in range(2)]
        n_att, n_skip, n_t, n_u = (part(FB, C) for _ in range(4))
        n_rz = sb("n_rz", [P, FB, H])
        n_s = sb("n_s", [P, 7, FB])
        n_bn = sb("n_bn", [P, FB, 6])
        n_mv = sb("n_mv", [P, FB, 2])
        eps_t = sb("eps_t", [P, 1])

        w_ld = sem("w_ld")
        ix_ld = sem("ix_ld")
        dst_ld = sem("dst_ld")
        iota_ok = sem("iota_ok")
        zeros_ok = sem("zeros_ok")
        eps_ok = sem("eps_ok")
        ident_ok = sem("ident_ok")
        row_cast = sem("row_cast")
        gate_ok = sem("gate_ok")
        bq_ok = sem("bq_ok")
        w_ok = sem("w_ok")
        xt_ld = [sem(f"xt_ld{s}") for s in range(TSLOTS)]
        tab_mm = sem("tab_mm")
        tab_ev = sem("tab_ev")
        tab_st = [sem(f"tab_st{s}") for s in range(TSLOTS)]
        zero_st = sem("zero_st")
        setup = sem("setup")
        first_mm = sem("first_mm")
        rel_st = sem("rel_st")
        bad_ok = sem("bad_ok")
        flag_ok = sem("flag_ok")
        low_ok = sem("low_ok")
        wide_steps = sem("wide_steps")
        spread_ok = sem("spread_ok")
        wide_ok = sem("wide_ok")

        ea_ld = [sem(f"ea_ld{p}") for p in range(2)]
        row_ld = [sem(f"row_ld{p}") for p in range(2)]
        qw_ld = [sem(f"qw_ld{p}") for p in range(2)]
        kv_ld = [sem(f"kv_ld{s}") for s in range(4)]
        idx_ok = sem("idx_ok")
        row_ok = sem("row_ok")
        e_ok = sem("e_ok")
        q_ok = sem("q_ok")
        topT_ok = sem("topT_ok")
        maxb_ok = sem("maxb_ok")
        sum_ok = sem("sum_ok")
        dist_ok = sem("dist_ok")
        hotne_ok = sem("hotne_ok")
        disten_ok = sem("disten_ok")
        negm_ok = sem("negm_ok")
        fade_ok = sem("fade_ok")
        exp_ok = sem("exp_ok")
        sums_ok = sem("sums_ok")
        kve_ok = sem("kve_ok")
        prod_ok = sem("prod_ok")
        logit_ok = sem("logit_ok")
        top_ok = sem("top_ok")
        negp_ok = sem("negp_ok")
        max_ok = sem("max_ok")
        hoten_ok = sem("hoten_ok")
        wv_ok = sem("wv_ok")
        shift_ok = sem("shift_ok")
        sums_st = sem("sums_st")

        n_ld = [sem(f"n_ld{p}") for p in range(2)]
        g_low_ok = sem("g_low_ok")
        g_init = sem("g_init")
        g_io = [sem(f"g_io{k}") for k in range(2)]
        g_ld = sem("g_ld")
        g_idx_ok = sem("g_idx_ok")
        g_get = [sem(f"g_get{k}") for k in range(4)]
        g_go = sem("g_go")
        g_pe = sem("g_pe")
        g_dve = sem("g_dve")
        g_act = sem("g_act")
        slot_free = sem("slot_free")
        store_free = sem("store_free")
        stats_in = sem("stats_in")
        n_mm = sem("n_mm")
        n_dve = sem("n_dve")
        n_act = sem("n_act")
        n_out = [sem(f"n_out{p}") for p in range(2)]

        block = ctx.enter_context(nc.Block())

        kv_rows = kv_tab.rearrange("(b p) c -> p b c", p=P)
        q_rows = q_tab.rearrange("(b p) c -> p b c", p=P)
        sum_rows = sum_tab.rearrange("(b p) c -> p b c", p=P)
        x_rows = x.rearrange("(b p) c -> p b c", p=P)
        out_rows = out.rearrange("(b p) c -> p b c", p=P)
        dst_line = dst.rearrange("(one e) -> one e", one=1)
        sum_zero = sum_tab.rearrange("(p j) c -> p (j c)", p=P)

        tab_rounds = BLOCKS // TB // TSLOTS
        loops = PAIRS // 2
        tab_banks = [e_ps[0], e_ps[1], q_ps[0]]
        G_OWN, G_EXP, G_WV, G_DVE = 4, 18, 20, 23
        N_BIAS, N_GATE, N_VAR1, N_VAR2, N_DVE = 4, 8, 15, 23, 25

        @block.sync
        def _(sp):
            for k, name in enumerate(("Wk", "Wv", "Wq")):
                sp.dma_start(w_kvq[:, k * C:(k + 1) * C], w[name]).then_inc(w_ld, 16)
            for k, name in enumerate(("bk", "bv", "bq")):
                sp.dma_start(b_kvq[:, k * C:(k + 1) * C], w[name].partition_broadcast(P)).then_inc(w_ld, 16)
            sp.dma_start(dst_all[:, :], dstT).then_inc(dst_ld, 16)
            sp.dma_start(dst_rows, dst.rearrange("(p j) -> p j", j=2 * PAIR)).then_inc(dst_ld, 16)

            def table_load(i, j):
                sp.dma_start(xt_buf[:, j, :], xT[:, bass.ds((i * TSLOTS + j) * (TB * P), TB * P)]
                             ).then_inc(xt_ld[j], 16)

            def table_store(i, j):
                sp.wait_ge(tab_ev, (i * TSLOTS + j + 1) * TB)
                rows = bass.ds((i * TSLOTS + j) * TB, TB)
                sp.dma_start(kv_rows[:, rows, :], tab_buf[:, j, :, 0:2 * C]).then_inc(tab_st[j], 16)
                sp.dma_start(q_rows[:, rows, :], tab_buf[:, j, :, 2 * C:3 * C]).then_inc(tab_st[j], 16)

            for j in range(TSLOTS):
                table_load(0, j)
            sp.dma_start(src_all[:, :], srcT).then_inc(ix_ld, 16)
            sp.dma_start(we[:, :], w["We"]).then_inc(w_ld, 16)
            sp.dma_start(wskip[:, :], w["Wskip"]).then_inc(w_ld, 16)
            for t, name in ((bskip, "bskip"), (gamma, "ln_gamma"), (beta_ln, "ln_beta")):
                sp.dma_start(t[:, :], w[name].partition_broadcast(P)).then_inc(w_ld, 16)
            sp.dma_start(wbeta[:, :, :].rearrange("p a c -> p (a c)"), w["Wbeta"].partition_broadcast(P)
                         ).then_inc(w_ld, 16)
            sp.wait_ge(zeros_ok, 1)
            for k in range(ZERO_DMAS):
                sp.dma_start(sum_zero[:, k * ZERO_W:(k + 1) * ZERO_W], zeros[:, :]).then_inc(zero_st, 16)
            sp.wait_ge(row_cast, 1)
            sp.dma_start(rel_row.rearrange("one (p j) -> (one p) j", j=2 * PAIR), rel_rows[:, :]
                         ).then_inc(rel_st, 16)
            with sp.Fori(0, tab_rounds - 1) as i:
                for j in range(TSLOTS):
                    table_store(i, j)
                    table_load(i + 1, j)
            for j in range(TSLOTS):
                table_store(tab_rounds - 1, j)
            for j in range(TSLOTS):
                sp.wait_ge(tab_st[j], 32 * tab_rounds)
            sp.wait_ge(rel_st, 16)
            sp.wait_ge(zero_st, 16 * ZERO_DMAS)
            sp.wait_ge(flag_ok, 1)
            grouped = sp.value_load(flag[0:1, 0:1], min_val=0, max_val=1)

            def window(g):
                return sp.value_load(dst_line[:, bass.ds(g * EDGES_G, 1)], min_val=0, max_val=N_NODES)

            def load(q, par, reuse):
                if reuse:
                    sp.wait_ge(e_ok, 2 * q - 2)
                    sp.wait_ge(row_ok, 2 * q - 2)
                    sp.wait_ge(q_ok, 2 * q - 2)
                sp.dma_start(ea[:, par, :], eaT[:, bass.ds(q * PAIR, PAIR)]).then_inc(ea_ld[par], 16)
                sp.dma_start(row[:, par, :], rel_row[:, bass.ds(q * PAIR, PAIR)]).then_inc(row_ld[par], 16)
                for u in range(2):
                    sp.dma_start(q_win[:, 2 * par + u, :], q_tab[bass.ds(window(2 * q + u), P), :]
                                 ).then_inc(qw_ld[par], 16)

            def store(q, par, ordered=(True, True)):
                for u in range(2):
                    g = 2 * q + u
                    w0 = window(g)
                    if not ordered[u]:
                        sp.wait_ge(sums_ok, g + 2)
                    else:
                        sp.wait_ge(sums_st, 16 * g)
                        sp.sem_inc(store_free, 1)
                        sp.wait_ge(sums_ok, g + 2)
                        sp.sem_inc(store_free, 1)
                    sp.dma_start(sum_tab[bass.ds(w0, P), :], sums[:, 2 * par + u, :]).then_inc(sums_st, 16)

            with sp.If(grouped):
                load(0, 0, False)
                load(1, 1, False)
                load(2, 0, True)
                load(3, 1, True)
                load(4, 0, True)
                store(0, 0, (False, True))
                load(5, 1, True)
                store(1, 1)
                with sp.Fori(3, loops) as i:
                    load(2 * i, 0, True)
                    store(2 * i - 4, 0)
                    load(2 * i + 1, 1, True)
                    store(2 * i - 3, 1)
                for q in range(PAIRS - 4, PAIRS):
                    store(q, q % 2)
                sp.wait_ge(sums_st, 16 * GROUPS)
            sp.wait_ge(wide_ok, 1)
            general = sp.value_load(wide[0:1, 0:1], min_val=0, max_val=1)
            with sp.If(general):
                for k in range(ZERO_DMAS):
                    sp.dma_start(sum_zero[:, k * ZERO_W:(k + 1) * ZERO_W], zeros[:, :]).then_inc(g_init, 16)
                sp.wait_ge(g_low_ok, 1)
                sp.dma_start(max_tab.rearrange("(p j) h -> p (j h)", p=P), g_low).then_inc(g_init, 16)

                def tile_load(t):
                    sp.dma_start(g_ea, eaT[:, bass.ds(t * P, P)]).then_inc(g_ld, 16)
                    sp.dma_start(g_dst, dst_line[:, bass.ds(t * P, P)].to_broadcast([P, P])).then_inc(g_ld, 16)

                tile_load(0)
                with sp.Fori(1, TILES) as t:
                    for k in range(2):
                        sp.wait_ge(g_io[k], 16 * t)
                    tile_load(t)
                sp.wait_ge(g_init, 16 * (ZERO_DMAS + 1))
                for k in range(2):
                    sp.wait_ge(g_io[k], 16 * TILES)

            def node_load(b, p):
                blocks = bass.ds(b * FB, FB)
                sp.dma_start(n_sum[p], sum_rows[:, blocks, :]).then_inc(n_ld[p], 16)
                sp.dma_start(n_x[p], x_rows[:, blocks, :]).then_inc(n_ld[p], 16)
                sp.dma_start(n_xt[p], xT[:, bass.ds(b * (FB * P), FB * P)]).then_inc(n_ld[p], 16)

            def node_store(b, p):
                sp.wait_ge(n_dve, N_DVE * (b + 1))
                sp.dma_start(out_rows[:, bass.ds(b * FB, FB), :], n_y[p]).then_inc(n_out[p], 16)

            batches = OUT_BLOCKS // FB
            node_load(0, 0)
            node_load(1, 1)
            with sp.Fori(0, batches // 2 - 1) as i:
                node_store(2 * i, 0)
                node_load(2 * i + 2, 0)
                node_store(2 * i + 1, 1)
                node_load(2 * i + 3, 1)
            node_store(batches - 2, 0)
            node_store(batches - 1, 1)
            for p in range(2):
                sp.wait_ge(n_out[p], 16 * (batches // 2))

        @block.gpsimd
        def _(pool):
            pool.memset(zeros[:, :], 0.0).then_inc(zeros_ok, 1)
            pool.memset(eps_t[:, :], EPS).then_inc(eps_ok, 1)
            pool.iota(iota_pn[:, :], [[-1, P]], base=0, channel_multiplier=1,
                      allow_small_or_imprecise_dtypes=True).then_inc(iota_ok, 1)
            pool.iota(iota_n[:, :], [[1, P]], base=0, channel_multiplier=0,
                      allow_small_or_imprecise_dtypes=True).then_inc(iota_ok, 1)
            pool.iota(neg_p[:, :], [[0, 1]], base=0, channel_multiplier=-1,
                      allow_small_or_imprecise_dtypes=True).then_inc(iota_ok, 1)
            pool.wait_ge(setup, 9)
            pool.partition_all_reduce(bad_all[:, :], bad[:, 3:4], P, RMAX).then_inc(bad_ok, 1)
            pool.wait_ge(flag_ok, 1)
            grouped = pool.value_load(flag[0:1, 0:1], min_val=0, max_val=1)
            pool.wait_ge(ix_ld, 16)
            for j in range(TSLOTS):
                pool.wait_ge(tab_st[j], 32 * tab_rounds)

            def gather(q, par, i, reuse):
                if reuse:
                    for u in range(2):
                        pool.wait_ge(kv_ld[2 * par + u], 16 * TILES_G * i)
                pool.tensor_copy(idx[:, par, :], src_all[:, bass.ds(q * TILES_Q, TILES_Q)]).then_inc(idx_ok, 1)
                pool.wait_ge(idx_ok, q + 1)
                if reuse:
                    pool.sem_inc(slot_free, 1)
                for u in range(2):
                    s = 2 * par + u
                    if reuse:
                        pool.wait_ge(kve_ok, 2 * q + u - 3)
                        pool.sem_inc(slot_free, 1)
                    for t in range(TILES_G):
                        pool.indirect_dma_start(
                            out=kv[:, s, t, :], out_offset=None, in_=kv_tab[:, :],
                            in_offset=bass.IndirectOffsetOnAxis(
                                ap=idx[:, par, u * TILES_G + t:u * TILES_G + t + 1], axis=0),
                        ).then_inc(kv_ld[s], 16)

            with pool.If(grouped):
                gather(0, 0, 0, False)
                gather(1, 1, 0, False)
                with pool.Fori(1, loops) as i:
                    gather(2 * i, 0, i, True)
                    gather(2 * i + 1, 1, i, True)
            pool.wait_ge(wide_steps, 2)
            pool.partition_all_reduce(spread[:, 2:4], spread[:, 0:2], P, RMAX).then_inc(spread_ok, 1)
            pool.wait_ge(wide_ok, 1)
            general = pool.value_load(wide[0:1, 0:1], min_val=0, max_val=1)
            with pool.If(general):

                def tile_rows(t):
                    pool.sem_inc(g_go, 1)
                    pool.tensor_copy(g_idx[:, 0:1], src_all[:, bass.ds(t, 1)]).then_inc(g_idx_ok, 1)
                    pool.tensor_copy(g_idx[:, 1:2], dst_all[:, bass.ds(t, 1)]).then_inc(g_idx_ok, 1)
                    pool.wait_ge(g_idx_ok, 2 * t + 2)
                    pool.sem_inc(g_go, 1)
                    for k, (to, table, col) in enumerate(((g_kv, kv_tab, 0), (g_q, q_tab, 1), (g_old, sum_tab, 1),
                                                          (g_old_max[:, :], max_tab, 1))):
                        pool.indirect_dma_start(
                            out=to, out_offset=None, in_=table[:, :],
                            in_offset=bass.IndirectOffsetOnAxis(ap=g_idx[:, col:col + 1], axis=0),
                        ).then_inc(g_get[k], 16)
                    pool.wait_ge(g_dve, G_DVE * (t + 1))
                    pool.sem_inc(g_go, 1)
                    for k, (table, of) in enumerate(((sum_tab, g_new), (max_tab, g_max[:, :]))):
                        pool.indirect_dma_start(
                            out=table[:, :], out_offset=bass.IndirectOffsetOnAxis(ap=g_put[:, :], axis=0),
                            in_=of, in_offset=None, bounds_check=ROWS - 1, oob_is_err=False,
                        ).then_inc(g_io[k], 16)

                pool.wait_ge(g_init, 16 * (ZERO_DMAS + 1))
                tile_rows(0)
                with pool.Fori(1, TILES) as t:
                    for k in range(2):
                        pool.wait_ge(g_io[k], 16 * t)
                    tile_rows(t)

        @block.tensor
        def _(pe):
            pe.wait_ge(setup, 2)
            pe.matmul(max_ps[:, 0:GROUPS], ones_f[:, :], first[:, :], start=True, stop=True).then_inc(first_mm, 1)
            pe.wait_ge(w_ok, 1)

            def table_step(i, j, reuse):
                pe.wait_ge(xt_ld[j], 16 * (i + 1))
                for b in range(TB):
                    if reuse:
                        pe.wait_ge(tab_ev, (i * TSLOTS + j - 1) * TB + b + 1)
                    pe.matmul(tab_banks[b][:, 0:3 * C], xt_buf[:, j, b * P:(b + 1) * P], w_kvq[:, :],
                              start=True, stop=True).then_inc(tab_mm, 1)

            for j in range(TSLOTS):
                table_step(0, j, j > 0)
            with pe.Fori(1, tab_rounds) as i:
                for j in range(TSLOTS):
                    table_step(i, j, True)
            pe.wait_ge(flag_ok, 1)
            grouped = pe.value_load(flag[0:1, 0:1], min_val=0, max_val=1)
            pe.wait_ge(tab_ev, BLOCKS)

            def row_and_e(q, par, u, i, first_use):
                g = 2 * q + u
                if u == 0:
                    pe.wait_ge(row_ld[par], 16 * (i + 1))
                if not (first_use and par == 0 and u == 0):
                    pe.wait_ge(dist_ok, g)
                pe.matmul(row_ps[:, :], ones_b[:, :], row[:, par, u * EDGES_G:(u + 1) * EDGES_G],
                          start=True, stop=True).then_inc(row_ok, 1)
                if u == 0:
                    pe.wait_ge(ea_ld[par], 16 * (i + 1))
                if not (first_use and par == 0):
                    pe.wait_ge(kve_ok, g - 1)
                for t in range(TILES_G):
                    mm = pe.matmul(e_ps[u][:, t * P:(t + 1) * P],
                                   ea[:, par, (u * TILES_G + t) * P:(u * TILES_G + t + 1) * P], we[:, :],
                                   start=True, stop=True)
                mm.then_inc(e_ok, 1)

            def q_spread(q, par, u, i, first_use):
                g = 2 * q + u
                if u == 0:
                    pe.wait_ge(qw_ld[par], 32 * (i + 1))
                pe.wait_ge(hotne_ok, g + 1)
                if not (first_use and par == 0):
                    pe.wait_ge(prod_ok, g - 1)
                for t in range(TILES_G):
                    mm = pe.matmul(q_ps[u][:, t * P:(t + 1) * P], hot_ne[:, u, t * P:(t + 1) * P],
                                   q_win[:, 2 * par + u, :], start=True, stop=True)
                mm.then_inc(q_ok, 1)

            def top_row(q, first_use=False):
                pe.wait_ge(top_ok, q + 1)
                if not first_use:
                    pe.wait_ge(negp_ok, q)
                pe.transpose(max_ps[0:1, 0:P], top[:, :], ident[:, :]).then_inc(topT_ok, 1)

            def max_spread(q, first_use=False):
                pe.wait_ge(max_ok, q + 2)
                if not first_use:
                    pe.wait_ge(negm_ok, q)
                pe.matmul(max_ps[:, 256:258], ones_f[:, :], neg_max[:, :], start=True, stop=True).then_inc(maxb_ok, 1)

            def node_sums(q, par, u, first_use=False):
                g = 2 * q + u
                s = 2 * par + u
                pe.wait_ge(hoten_ok, g + 1)
                pe.wait_ge(wv_ok, g + 1)
                if not first_use:
                    pe.wait_ge(sums_ok, g)
                for t in range(TILES_G):
                    pe.matmul(sum_ps[u][:, 0:AC], hot_en[:, s, t, :], wv[:, s, t, :], start=(t == 0), stop=False)
                pe.wait_ge(shift_ok, g + 1)
                pe.wait_ge(sums_ok, g + 1)
                pe.matmul(sum_ps[u][:, 0:AC], shift[:, u, :], sums[:, (s + 3) % 4, :],
                          start=False, stop=True).then_inc(sum_ok, 1)

            def step(q, par, i, first_use=False):
                before = not (first_use and par == 0)
                row_and_e(q, par, 0, i, first_use)
                if before:
                    top_row(q - 1, first_use)
                row_and_e(q, par, 1, i, first_use)
                if before:
                    max_spread(q - 1, first_use)
                q_spread(q, par, 0, i, first_use)
                q_spread(q, par, 1, i, first_use)
                if before:
                    node_sums(q - 1, 1 - par, 0, first_use)
                    node_sums(q - 1, 1 - par, 1, first_use)

            with pe.If(grouped):
                step(0, 0, 0, True)
                step(1, 1, 0, True)
                with pe.Fori(1, loops) as i:
                    step(2 * i, 0, i)
                    step(2 * i + 1, 1, i)
                top_row(PAIRS - 1)
                max_spread(PAIRS - 1)
                node_sums(PAIRS - 1, 1, 0)
                node_sums(PAIRS - 1, 1, 1)

            pe.wait_ge(wide_ok, 1)
            general = pe.value_load(wide[0:1, 0:1], min_val=0, max_val=1)
            with pe.If(general):
                with pe.Fori(0, TILES) as t:
                    pe.wait_ge(g_ld, 32 * t + 32)
                    pe.matmul(e_ps[0][:, 0:C], g_ea, we[:, :], start=True, stop=True).then_inc(g_pe, 1)
                    pe.wait_ge(g_dve, G_DVE * t + G_OWN)
                    for h in range(H):
                        mm = pe.matmul(q_ps[h // 4][:, (h % 4) * P:(h % 4 + 1) * P], g_own[:, h, :], ident[:, :],
                                       start=True, stop=True)
                    mm.then_inc(g_pe, 1)
                    pe.wait_ge(g_dve, G_DVE * t + G_WV)
                    pe.matmul(sum_ps[0][:, 0:AC], g_same, g_wv, start=True, stop=True).then_inc(g_pe, 1)

            def skip_project(b, p, i, reuse):
                pe.wait_ge(n_ld[p], 48 * (i + 1))
                if reuse:
                    pe.wait_ge(n_dve, N_DVE * (b - 1) + N_BIAS)
                for k in range(FB):
                    mm = pe.matmul(e_ps[k // 4][:, (k % 4) * P:(k % 4 + 1) * P], n_xt[p][:, k * P:(k + 1) * P],
                                   wskip[:, :], start=True, stop=True)
                mm.then_inc(n_mm, 1)

            skip_project(0, 0, 0, False)
            skip_project(1, 1, 0, True)
            with pe.Fori(1, OUT_BLOCKS // FB // 2) as i:
                skip_project(2 * i, 0, i, True)
                skip_project(2 * i + 1, 1, i, True)

        @block.scalar
        def _(act):
            act.wait_ge(flag_ok, 1)
            grouped = act.value_load(flag[0:1, 0:1], min_val=0, max_val=1)
            act.wait_ge(iota_ok, 3)
            act.wait_ge(setup, 7)

            def one_hot(q, par, u, first_use):
                g = 2 * q + u
                act.wait_ge(row_ok, g + 1)
                if not (first_use and par == 0):
                    act.wait_ge(hotne_ok, g - 1)
                act.activation(dist[:, u, :], row_ps[:, :], ACT.Abs, bias=neg_p[:, :]).then_inc(dist_ok, 1)
                act.wait_ge(dist_ok, g + 1)
                if not (first_use and par == 0):
                    act.wait_ge(q_ok, g - 1)
                act.activation(hot_ne[:, u, :], dist[:, u, :], ACT.Relu, bias=1.0, scale=-1.0).then_inc(hotne_ok, 1)

            def edge_one_hot(q, par, u, reuse, first_use=False):
                g = 2 * q + u
                s = 2 * par + u
                if not (first_use and par == 0):
                    act.wait_ge(hoten_ok, g - 1)
                for t in range(TILES_G):
                    last = act.activation(dist_en[:, u, t, :], iota_n[:, :], ACT.Abs,
                                          bias=neg_rel[:, bass.ds(g * TILES_G + t, 1)])
                last.then_inc(disten_ok, 1)
                act.wait_ge(disten_ok, g + 1)
                if reuse:
                    act.wait_ge(sum_ok, g - 3)
                act.activation(hot_en[:, s, :, :], dist_en[:, u, :, :], ACT.Relu, bias=1.0, scale=-1.0
                               ).then_inc(hoten_ok, 1)

            def weights(q, par, first_use=False):
                act.wait_ge(maxb_ok, q + 1)
                if not first_use:
                    act.wait_ge(exp_ok, q)
                    act.wait_ge(fade_ok, q)
                act.copy(neg_max_b[:, :], max_ps[:, 256:258]).then_inc(negm_ok, 1)
                act.wait_ge(negm_ok, q + 1)
                act.wait_ge(logit_ok, 2 * q + 2)
                if reused[0]:
                    act.wait_ge(sum_ok, 2 * q - 2)
                act.activation(wv[:, 2 * par:2 * par + 2, :, C:AC].rearrange("p a t h -> p (a t) h"),
                               logit[:, bass.ds(q * (TILES_Q * H), TILES_Q * H)].rearrange("p (t h) -> p t h", h=H),
                               ACT.Exp, bias=neg_max_b[:, par:par + 1]).then_inc(exp_ok, 1)
                if reused[0]:
                    act.wait_ge(shift_ok, 2 * q - 3)
                act.activation(fade[:, par:par + 1], neg_max_b[:, 1 - par:2 - par], ACT.Exp, scale=-1.0,
                               bias=neg_max_b[:, par:par + 1]).then_inc(fade_ok, 1)

            def sums_out(q, par, u):
                g = 2 * q + u
                act.wait_ge(sum_ok, g + 1)
                if reused[0]:
                    act.wait_ge(sums_st, 16 * (g - 3))
                act.copy(sums[:, 2 * par + u, :], sum_ps[u][:, 0:AC]).then_inc(sums_ok, 1)

            reused = [False]

            def step(q, par, reuse=True, first_use=False):
                before = not (first_use and par == 0)
                one_hot(q, par, 0, first_use)
                one_hot(q, par, 1, first_use)
                if before:
                    weights(q - 1, 1 - par, first_use)
                edge_one_hot(q, par, 0, reuse, first_use)
                if before:
                    sums_out(q - 1, 1 - par, 0)
                edge_one_hot(q, par, 1, reuse, first_use)
                if before:
                    sums_out(q - 1, 1 - par, 1)

            with act.If(grouped):
                step(0, 0, False, True)
                step(1, 1, False, True)
                step(2, 0)
                reused[0] = True
                step(3, 1)
                with act.Fori(2, loops) as i:
                    step(2 * i, 0)
                    step(2 * i + 1, 1)
                weights(PAIRS - 1, 1)
                sums_out(PAIRS - 1, 1, 0)
                sums_out(PAIRS - 1, 1, 1)

            act.wait_ge(wide_ok, 1)
            general = act.value_load(wide[0:1, 0:1], min_val=0, max_val=1)
            with act.If(general):
                with act.Fori(0, TILES) as t:
                    act.wait_ge(g_dve, G_DVE * t + G_EXP)
                    act.activation(g_exp[:, :, :], g_exp[:, :, :], ACT.Exp).then_inc(g_act, 1)

            act.wait_ge(eps_ok, 1)
            with act.Fori(0, OUT_BLOCKS // FB) as b:
                act.wait_ge(n_dve, N_DVE * b + N_GATE)
                act.activation(n_s[:, 1, :], n_s[:, 0, :], ACT.Exp, scale=-1.0).then_inc(n_act, 1)
                act.wait_ge(n_dve, N_DVE * b + N_VAR1)
                act.activation(n_s[:, 3, :], n_mv[:, :, 1], ACT.Sqrt, bias=eps_t[:, :]).then_inc(n_act, 1)
                act.wait_ge(n_dve, N_DVE * b + N_VAR2)
                act.activation(n_s[:, 5, :], n_mv[:, :, 1], ACT.Sqrt, bias=eps_t[:, :]).then_inc(n_act, 1)

        @block.vector
        def _(dve):
            dve.memset(ones_f[:, :], 1.0)
            dve.memset(ones_b[:, :], 1.0)
            dve.memset(one_col[:, :], 1.0)
            dve.memset(neg_max[:, :], BIG).then_inc(max_ok, 1)
            dve.memset(sums[:, :, :], 0.0).then_inc(sums_ok, 1)
            dve.wait_ge(iota_ok, 2)
            dve.tensor_scalar(ident[:, :], iota_pn[:, :], 0.0, None, ALU.is_equal).then_inc(ident_ok, 1)
            dve.wait_ge(dst_ld, 32)
            dve.tensor_copy(first[:, :], dst_all[0:1, 0:TILES:TILES_G]).then_inc(setup, 1)
            dve.tensor_copy(dst_rows_f, dst_rows).then_inc(setup, 1)
            dve.tensor_copy(neg_rel[:, :], dst_all[:, :]).then_inc(setup, 1)
            dve.wait_ge(first_mm, 1)
            dve.tensor_copy(first_b[:, :], max_ps[:, 0:GROUPS]).then_inc(setup, 1)
            dve.wait_ge(setup, 4)
            rows4 = dst_rows_f.rearrange("p (g e) -> p g e", e=EDGES_G)
            dve.tensor_tensor(rel_rows[:, :].rearrange("p (g e) -> p g e", e=EDGES_G), rows4,
                              rows4[:, :, 0:1].to_broadcast([PAIRS // 2, 4, EDGES_G]),
                              ALU.subtract).then_inc(row_cast, 1)
            rel3 = neg_rel[:, :].rearrange("p (g t) -> p g t", t=TILES_G)
            dve.tensor_tensor(rel3, first_b[:, :].unsqueeze(2).to_broadcast([P, GROUPS, TILES_G]), rel3,
                              ALU.subtract).then_inc(setup, 1)
            dve.memset(delta[:, 0:1], 0.0).then_inc(setup, 1)
            dve.tensor_tensor(delta[:, 1:GROUPS], first_b[:, 1:GROUPS], first_b[:, 0:GROUPS - 1],
                              ALU.subtract).then_inc(setup, 1)
            dve.wait_ge(setup, 7)
            dve.tensor_reduce(bad[:, 0:1], neg_rel[:, :], AX_X, ALU.max).then_inc(low_ok, 1)
            dve.tensor_reduce(bad[:, 1:2], neg_rel[:, :], AX_X, ALU.min, negate=True).then_inc(low_ok, 1)
            dve.tensor_reduce(bad[:, 2:3], delta[:, :], AX_X, ALU.min, negate=True).then_inc(low_ok, 1)
            dve.wait_ge(low_ok, 3)
            dve.tensor_scalar(bad[:, 1:2], bad[:, 1:2], float(1 - P), None, ALU.add).then_inc(setup, 1)
            dve.wait_ge(setup, 8)
            dve.tensor_reduce(bad[:, 3:4], bad[:, 0:3], AX_X, ALU.max).then_inc(setup, 1)
            dve.wait_ge(w_ld, 16 * 12)
            dve.tensor_tensor(w_out[:, :], wbeta[:, 0, :], wbeta[:, 2, :], ALU.add).then_inc(gate_ok, 1)
            dve.tensor_tensor(w_skip[:, :], wbeta[:, 1, :], wbeta[:, 2, :], ALU.subtract).then_inc(gate_ok, 1)
            dve.tensor_scalar(b_kvq[:, 2 * C:3 * C], b_kvq[:, 2 * C:3 * C], D ** -0.5, None, ALU.mult).then_inc(bq_ok, 1)
            dve.tensor_scalar(w_kvq[:, 2 * C:3 * C], w_kvq[:, 2 * C:3 * C], D ** -0.5, None, ALU.mult).then_inc(w_ok, 1)
            dve.wait_ge(bad_ok, 1)
            dve.tensor_scalar(flag[:, :], bad_all[:, :], 0.0, None, ALU.is_le).then_inc(flag_ok, 1)
            dve.wait_ge(bq_ok, 1)

            def table_step(i, j, reuse):
                if reuse:
                    dve.wait_ge(tab_st[j], 32 * i)
                for b in range(TB):
                    dve.wait_ge(tab_mm, (i * TSLOTS + j) * TB + b + 1)
                    dve.tensor_tensor(tab_buf[:, j, b, :], tab_banks[b][:, 0:3 * C], b_kvq[:, :],
                                      ALU.add).then_inc(tab_ev, 1)

            for j in range(TSLOTS):
                table_step(0, j, False)
            with dve.Fori(1, tab_rounds) as i:
                for j in range(TSLOTS):
                    table_step(i, j, True)
            dve.wait_ge(flag_ok, 1)
            grouped = dve.value_load(flag[0:1, 0:1], min_val=0, max_val=1)

            def keys_values(q, par, u, i, reuse):
                g = 2 * q + u
                s = 2 * par + u
                dve.wait_ge(kv_ld[s], 16 * TILES_G * (i + 1))
                dve.wait_ge(e_ok, g + 1)
                if reuse:
                    dve.wait_ge(wv_ok, g - 3)
                e4 = e_ps[u][:, :].rearrange("p (t c) -> p t c", c=C).unsqueeze(2)
                dve.tensor_tensor(kve[:, s, :, :, :], kv[:, s, :, :].rearrange("p t (a c) -> p t a c", a=2),
                                  e4.to_broadcast([P, TILES_G, 2, C]), ALU.add).then_inc(kve_ok, 1)

            def products(q, par, u, first_use):
                g = 2 * q + u
                s = 2 * par + u
                dve.wait_ge(q_ok, g + 1)
                dve.wait_ge(kve_ok, g + 1)
                if not (first_use and par == 0):
                    dve.wait_ge(logit_ok, g - 1)
                dve.tensor_tensor(prod[:, u, :].rearrange("p (t c) -> p t c", c=C),
                                  q_ps[u][:, :].rearrange("p (t c) -> p t c", c=C),
                                  kve[:, s, :, 0, :], ALU.mult).then_inc(prod_ok, 1)

            def logits(q, par, u):
                g = 2 * q + u
                dve.wait_ge(prod_ok, g + 1)
                dve.tensor_reduce(logit[:, bass.ds(g * (TILES_G * H), TILES_G * H)],
                                  prod[:, u, :].rearrange("p (h d) -> p h d", d=D), AX_X, ALU.add).then_inc(logit_ok, 1)

            def pair_top(q, first_use=False):
                dve.wait_ge(logit_ok, 2 * q + 2)
                if not first_use:
                    dve.wait_ge(topT_ok, q)
                dve.tensor_reduce(top[:, :], logit[:, bass.ds(q * (TILES_Q * H), TILES_Q * H)], AX_X,
                                  ALU.max).then_inc(top_ok, 1)

            def pair_max(q, par, first_use=False):
                dve.wait_ge(topT_ok, q + 1)
                dve.tensor_reduce(neg_pair[:, :], max_ps[0:1, 0:P], AX_X, ALU.max, negate=True).then_inc(negp_ok, 1)
                dve.wait_ge(negp_ok, q + 1)
                dve.wait_ge(max_ok, q + 1)
                if not first_use:
                    dve.wait_ge(maxb_ok, q)
                dve.tensor_tensor(neg_max[:, par:par + 1], neg_max[:, 1 - par:2 - par], neg_pair[:, :],
                                  ALU.min).then_inc(max_ok, 1)

            def weighted(q, par, u, reuse):
                g = 2 * q + u
                s = 2 * par + u
                dve.wait_ge(exp_ok, q + 1)
                if reuse:
                    dve.wait_ge(sum_ok, g - 3)
                dve.tensor_tensor(wv[:, s, :, 0:C].rearrange("p t (h d) -> p t h d", d=D),
                                  kve[:, s, :, 1, :].rearrange("p t (h d) -> p t h d", d=D),
                                  wv[:, s, :, C:AC].unsqueeze(3).to_broadcast([P, TILES_G, H, D]),
                                  ALU.mult).then_inc(wv_ok, 1)

            def shifts(q, par, u, first_use=False):
                g = 2 * q + u
                if u == 0:
                    dve.wait_ge(fade_ok, q + 1)
                if not first_use:
                    dve.wait_ge(sum_ok, g - 1)
                dve.tensor_scalar(shift[:, u, :], iota_pn[:, :], delta[:, bass.ds(g, 1)],
                                  fade[:, par:par + 1] if u == 0 else one_col[:, :],
                                  ALU.is_equal, ALU.mult).then_inc(shift_ok, 1)

            def step(q, par, i, first_use=False, b_reuse=True):
                before = not (first_use and par == 0)
                keys_values(q, par, 0, i, not first_use)
                if before:
                    pair_max(q - 1, 1 - par, first_use)
                keys_values(q, par, 1, i, not first_use)
                if before:
                    weighted(q - 1, 1 - par, 0, b_reuse)
                    weighted(q - 1, 1 - par, 1, b_reuse)
                    shifts(q - 1, 1 - par, 0, first_use)
                    shifts(q - 1, 1 - par, 1, first_use)
                for u in range(2):
                    products(q, par, u, first_use)
                for u in range(2):
                    logits(q, par, u)
                pair_top(q, not before)

            with dve.If(grouped):
                step(0, 0, 0, True, False)
                step(1, 1, 0, True, False)
                step(2, 0, 1, False, False)
                step(3, 1, 1)
                with dve.Fori(2, loops) as i:
                    step(2 * i, 0, i)
                    step(2 * i + 1, 1, i)
                pair_max(PAIRS - 1, 1)
                weighted(PAIRS - 1, 1, 0, True)
                weighted(PAIRS - 1, 1, 1, True)
                shifts(PAIRS - 1, 1, 0)
                shifts(PAIRS - 1, 1, 1)
                dve.tensor_reduce(spread[:, 0:1], logit[:, :], AX_X, ALU.max).then_inc(wide_steps, 1)
                dve.tensor_reduce(spread[:, 1:2], logit[:, :], AX_X, ALU.min, negate=True).then_inc(wide_steps, 1)
            with dve.Else():
                dve.memset(spread[:, 0:2], BIG).then_inc(wide_steps, 2)
            dve.wait_ge(spread_ok, 1)
            dve.tensor_tensor(spread[:, 0:1], spread[:, 2:3], spread[:, 3:4], ALU.add).then_inc(wide_steps, 1)
            dve.wait_ge(wide_steps, 3)
            dve.tensor_scalar(wide[:, :], spread[:, 0:1], RANGE, 0.0, ALU.is_le, ALU.is_equal).then_inc(wide_ok, 1)
            dve.wait_ge(wide_ok, 1)
            general = dve.value_load(wide[0:1, 0:1], min_val=0, max_val=1)

            def general_tile(t):
                done = [0]

                def link(ins):
                    done[0] += 1
                    ins.then_inc(g_dve, 1)
                    dve.wait_ge(g_dve, G_DVE * t + done[0])

                dve.wait_ge(g_ld, 32 * t + 32)
                for k in range(4):
                    dve.wait_ge(g_get[k], 16 * t + 16)
                dve.wait_ge(g_pe, 3 * t + 1)
                link(dve.tensor_tensor(g_kve, g_kv.rearrange("p (a c) -> p a c", a=2),
                                       e_ps[0][:, 0:C].unsqueeze(1).to_broadcast([P, 2, C]), ALU.add))
                link(dve.tensor_tensor(g_prod, g_kve[:, 0, :], g_q, ALU.mult))
                link(dve.tensor_reduce(g_logit[:, :], g_prod.rearrange("p (h d) -> p h d", d=D), AX_X, ALU.add))
                link(dve.tensor_copy(g_own, g_logit[:, :].unsqueeze(2).to_broadcast([P, H, P])))
                assert done[0] == G_OWN
                link(dve.tensor_copy(g_dst_f, g_dst))
                link(dve.tensor_copy(g_node[:, 0:1], dst_all[:, bass.ds(t, 1)]))
                link(dve.tensor_scalar(g_same, g_dst_f, g_node[:, 0:1], None, ALU.is_equal))
                link(dve.tensor_scalar(g_apart, g_same, -1.0, BIG, ALU.add, ALU.mult))
                link(dve.scalar_tensor_tensor(g_before, iota_pn[:, :], 0.0, g_same, ALU.is_gt, ALU.mult))
                link(dve.tensor_reduce(g_node[:, 1:2], g_before, AX_X, ALU.max))
                link(dve.tensor_scalar(g_put[:, :], g_node[:, 1:2], float(ROWS), g_node[:, 0:1], ALU.mult, ALU.add))
                dve.wait_ge(g_pe, 3 * t + 2)
                link(dve.tensor_tensor(g_peers[:, 0:4, :], q_ps[0][:, :].rearrange("p (h e) -> p h e", e=P),
                                       g_same.unsqueeze(1).to_broadcast([P, 4, P]), ALU.mult))
                link(dve.tensor_tensor(g_peers[:, 4:H, :], q_ps[1][:, :].rearrange("p (h e) -> p h e", e=P),
                                       g_same.unsqueeze(1).to_broadcast([P, 4, P]), ALU.mult))
                link(dve.tensor_tensor(g_peers, g_peers, g_apart.unsqueeze(1).to_broadcast([P, H, P]), ALU.add))
                link(dve.tensor_reduce(g_max[:, :], g_peers, AX_X, ALU.max))
                link(dve.tensor_tensor(g_max[:, :], g_max[:, :], g_old_max[:, :], ALU.max))
                link(dve.tensor_tensor(g_exp[:, 0, :], g_logit[:, :], g_max[:, :], ALU.subtract))
                link(dve.tensor_tensor(g_exp[:, 1, :], g_old_max[:, :], g_max[:, :], ALU.subtract))
                assert done[0] == G_EXP
                dve.wait_ge(g_act, t + 1)
                link(dve.tensor_copy(g_wv[:, C:AC], g_exp[:, 0, :]))
                link(dve.tensor_tensor(g_wv[:, 0:C].rearrange("p (h d) -> p h d", d=D),
                                       g_kve[:, 1, :].rearrange("p (h d) -> p h d", d=D),
                                       g_exp[:, 0, :].unsqueeze(2).to_broadcast([P, H, D]), ALU.mult))
                assert done[0] == G_WV
                link(dve.tensor_tensor(g_old[:, 0:C].rearrange("p (h d) -> p h d", d=D),
                                       g_old[:, 0:C].rearrange("p (h d) -> p h d", d=D),
                                       g_exp[:, 1, :].unsqueeze(2).to_broadcast([P, H, D]), ALU.mult))
                link(dve.tensor_tensor(g_old[:, C:AC], g_old[:, C:AC], g_exp[:, 1, :], ALU.mult))
                dve.wait_ge(g_pe, 3 * t + 3)
                link(dve.tensor_tensor(g_new, sum_ps[0][:, 0:AC], g_old, ALU.add))
                assert done[0] == G_DVE

            with dve.If(general):
                dve.memset(g_low, -BIG).then_inc(g_low_ok, 1)
                with dve.Fori(0, TILES) as t:
                    general_tile(t)

            dve.wait_ge(gate_ok, 2)

            def spread_c(t):
                return t[:, :].unsqueeze(1).to_broadcast([P, FB, C])

            def spread_b(t):
                return t.unsqueeze(2).to_broadcast([P, FB, C])

            def nodes(b, p, i, reuse):
                done = [0]

                def link(ins):
                    done[0] += 1
                    ins.then_inc(n_dve, 1)
                    dve.wait_ge(n_dve, N_DVE * b + done[0])

                dve.wait_ge(n_ld[p], 48 * (i + 1))
                link(dve.tensor_scalar(n_rz[:, :, :], n_sum[p][:, :, C:AC], 1e-30, None, ALU.max))
                link(dve.reciprocal(n_rz[:, :, :], n_rz[:, :, :]))
                link(dve.tensor_tensor(n_att.rearrange("p b (h d) -> p b h d", d=D),
                                       n_sum[p][:, :, 0:C].rearrange("p b (h d) -> p b h d", d=D),
                                       n_rz[:, :, :].unsqueeze(3).to_broadcast([P, FB, H, D]), ALU.mult))
                dve.wait_ge(n_mm, b + 1)
                dve.tensor_tensor(n_skip[:, 0:4, :], e_ps[0][:, :].rearrange("p (k c) -> p k c", c=C),
                                  bskip[:, :].unsqueeze(1).to_broadcast([P, 4, C]), ALU.add)
                link(dve.tensor_tensor(n_skip[:, 4:FB, :], e_ps[1][:, 0:(FB - 4) * C].rearrange("p (k c) -> p k c", c=C),
                                       bskip[:, :].unsqueeze(1).to_broadcast([P, FB - 4, C]), ALU.add))
                assert done[0] == N_BIAS
                link(dve.tensor_tensor(n_t, n_att, spread_c(w_out), ALU.mult))
                link(dve.tensor_tensor(n_u, n_skip, spread_c(w_skip), ALU.mult))
                link(dve.tensor_tensor(n_t, n_t, n_u, ALU.add))
                link(dve.tensor_reduce(n_s[:, 0, :], n_t, AX_X, ALU.add))
                assert done[0] == N_GATE
                dve.wait_ge(n_act, 3 * b + 1)
                link(dve.tensor_scalar(n_s[:, 2, :], n_s[:, 1, :], 1.0, None, ALU.add))
                link(dve.reciprocal(n_s[:, 2, :], n_s[:, 2, :]))
                link(dve.tensor_tensor(n_u, n_skip, n_att, ALU.subtract))
                link(dve.tensor_tensor(n_u, n_u, spread_b(n_s[:, 2, :]), ALU.mult))
                link(dve.tensor_tensor(n_att, n_att, n_u, ALU.add))
                for k in range(FB):
                    last = dve.bn_stats(n_bn[:, k, :], n_att[:, k, :])
                link(last)
                dve.sem_inc(stats_in, 1)
                for k in range(FB):
                    last = dve.bn_aggr(n_mv[:, k, :], n_bn[:, k, :])
                link(last)
                assert done[0] == N_VAR1
                dve.wait_ge(n_act, 3 * b + 2)
                link(dve.reciprocal(n_s[:, 4, :], n_s[:, 3, :]))
                for k in range(FB):
                    last = dve.tensor_scalar(n_t[:, k, :], n_att[:, k, :], n_mv[:, k, 0:1], n_s[:, 4, k:k + 1],
                                             ALU.subtract, ALU.mult)
                link(last)
                link(dve.tensor_tensor(n_t, n_t, spread_c(gamma), ALU.mult))
                link(dve.tensor_tensor(n_t, n_t, spread_c(beta_ln), ALU.add))
                link(dve.scalar_tensor_tensor(n_u, n_t, 0.0, n_x[p], ALU.max, ALU.add))
                link(dve.tensor_tensor(n_u, n_u, n_x[p], ALU.add))
                for k in range(FB):
                    last = dve.bn_stats(n_bn[:, k, :], n_u[:, k, :])
                link(last)
                dve.sem_inc(stats_in, 1)
                for k in range(FB):
                    last = dve.bn_aggr(n_mv[:, k, :], n_bn[:, k, :])
                link(last)
                assert done[0] == N_VAR2
                dve.wait_ge(n_act, 3 * b + 3)
                link(dve.reciprocal(n_s[:, 6, :], n_s[:, 5, :]))
                if reuse:
                    dve.wait_ge(n_out[p], 16 * i)
                for k in range(FB):
                    last = dve.tensor_scalar(n_y[p][:, k, :], n_u[:, k, :], n_mv[:, k, 0:1], n_s[:, 6, k:k + 1],
                                             ALU.subtract, ALU.mult)
                link(last)
                assert done[0] == N_DVE

            nodes(0, 0, 0, False)
            nodes(1, 1, 0, False)
            with dve.Fori(1, OUT_BLOCKS // FB // 2) as i:
                nodes(2 * i, 0, i, True)
                nodes(2 * i + 1, 1, i, True)


_WEIGHTS = ("Wq", "bq", "Wk", "bk", "Wv", "bv", "We", "Wskip", "bskip", "Wbeta", "ln_gamma", "ln_beta")


def kernel(**inputs):
    import numpy as np
    import concourse.bacc as bacc
    from concourse.bass_utils import run_bass_kernel_spmd

    x = np.zeros((ROWS, C), np.float32)
    x[:N_NODES] = inputs["x"]
    ea = np.zeros((C, EDGES), np.float32)
    ea[:, :N_EDGES] = np.asarray(inputs["edge_attr_128"]).T
    src = np.zeros(EDGES, np.int32)
    src[:N_EDGES] = inputs["src"]
    dst = np.full(EDGES, N_NODES, np.int32)
    dst[:N_EDGES] = inputs["dst"]
    arrays = {
        "x": x, "xT": np.ascontiguousarray(x.T), "eaT": ea,
        "srcT": np.ascontiguousarray(src.reshape(TILES, P).T),
        "dstT": np.ascontiguousarray(dst.reshape(TILES, P).T),
        "dst": dst,
    }
    for name in _WEIGHTS:
        a = np.ascontiguousarray(inputs["L0_gnn_" + name])
        arrays["w_" + name] = a.reshape(-1) if name == "Wbeta" else a

    nc = bacc.Bacc("TRN2", target_bir_lowering=False, num_devices=1)
    aps = {n: nc.dram_tensor(n, a.shape, mybir.dt.from_np(a.dtype), kind="ExternalInput").ap()
           for n, a in arrays.items()}
    out = nc.dram_tensor("out", (OUT_BLOCKS * P, C), F32, kind="ExternalOutput").ap()
    build(nc, aps["xT"], aps["x"], aps["eaT"], aps["srcT"], aps["dstT"], aps["dst"],
          {n: aps["w_" + n] for n in _WEIGHTS}, out)
    r = run_bass_kernel_spmd(nc, [arrays], core_ids=[0])
    return r.results[0]["out"][:N_NODES]
```

```python
from contextlib import ExitStack

import concourse.bass as bass
from concourse import mybir

F32 = mybir.dt.float32
BF16 = mybir.dt.bfloat16
I32 = mybir.dt.int32
ALU = mybir.AluOpType
ACT = mybir.ActivationFunctionType
AX_X = mybir.AxisListType.X
RMAX = bass.bass_isa.ReduceOp.max

P = 128
H = 8
D = 16
C = H * D
N_NODES = 12500
N_EDGES = 200000
TILES_G = 4
EDGES_G = TILES_G * P
TILES_Q = 2 * TILES_G
PAIRS = 2 * -(-N_EDGES // (4 * EDGES_G))
GROUPS = 2 * PAIRS
TILES = GROUPS * TILES_G
EDGES = TILES * P
BLOCKS = 99
ROWS = BLOCKS * P
OUT_BLOCKS = 98
AC = C + H
PAIR = TILES_Q * P
EPS = 1e-5
RANGE = 60.0
BIG = 1e30

TB = 3
TSLOTS = 3
FB = 7
ROUND = 4
KVQ_DMAS = 6
W_DMAS = 6
ZERO_DMAS = 11
ZERO_W = BLOCKS * AC // ZERO_DMAS


def build(nc, xT, x, eaT, srcT, dstT, dst, w, out):
    ctx = ExitStack()
    with ctx:
        def sb(name, shape, dt=F32):
            return ctx.enter_context(nc.sbuf_tensor(name, shape, dt))

        def ps(name, shape):
            return ctx.enter_context(nc.psum_tensor(name, shape, F32))

        def sem(name):
            return ctx.enter_context(nc.semaphore(name))

        kv_tab = nc.dram_tensor("kv_tab", (ROWS, 2 * C), F32).ap()
        q_tab = nc.dram_tensor("q_tab", (ROWS, C), F32).ap()
        sum_tab = nc.dram_tensor("sum_tab", (ROWS, AC), F32).ap()
        max_tab = nc.dram_tensor("max_tab", (ROWS, H), F32).ap()
        rel_row = nc.dram_tensor("rel_row", (1, EDGES), BF16).ap()

        e_ps = [ps(f"e_ps{u}", [P, 512]) for u in range(2)]
        q_ps = [ps(f"q_ps{u}", [P, 512]) for u in range(2)]
        sum_ps = [ps(f"sum_ps{u}", [P, 512]) for u in range(2)]
        row_ps = ps("row_ps", [P, 512])
        max_ps = ps("max_ps", [P, 512])

        w_kvq = sb("w_kvq", [P, 3 * C])
        b_kvq = sb("b_kvq", [P, 3 * C])
        we = sb("we", [P, C])
        wskip = sb("wskip", [P, C + 1])
        skip_row = sb("skip_row", [1, C + 1])
        skip_junk = sb("skip_junk", [P, C])
        bskip = sb("bskip", [P, C])
        wbeta = sb("wbeta", [P, 3, C])
        w_out = sb("w_out", [P, C])
        w_skip = sb("w_skip", [P, C])
        gamma = sb("gamma", [P, C])
        beta_ln = sb("beta_ln", [P, C])
        ident = sb("ident", [P, P])
        ones_f = sb("ones_f", [1, P])
        ones_b = sb("ones_b", [1, P], BF16)
        iota_n = sb("iota_n", [P, P])
        iota_pn = sb("iota_pn", [P, P])
        neg_p = sb("neg_p", [P, 1])
        zeros = sb("zeros", [P, ZERO_W])
        one_col = sb("one_col", [P, 1])

        xt_buf = sb("xt_buf", [P, TSLOTS, TB * P])
        tab_buf = sb("tab_buf", [P, TSLOTS, TB, 3 * C])

        src_all = sb("src_all", [P, TILES], I32)
        dst_all = sb("dst_all", [P, TILES], I32)
        neg_rel = sb("neg_rel", [P, TILES])
        first = sb("first", [1, GROUPS])
        first_b = sb("first_b", [P, GROUPS])
        delta = sb("delta", [P, GROUPS])
        rel_rows = sb("rel_rows", [PAIRS // 2, 2 * PAIR], BF16)
        bad = sb("bad", [P, 4])
        bad_all = sb("bad_all", [P, 1])
        flag = sb("flag", [P, 1], I32)
        lows = sb("lows", [P, PAIRS])
        spread = sb("spread", [P, 4])
        wide = sb("wide", [P, 1], I32)

        idx = sb("idx", [P, 2, TILES_Q], I32)
        kv = sb("kv", [P, 4, TILES_G, 2 * C])
        ea = sb("ea", [P, 2, 2 * EDGES_G])
        row = sb("row", [1, 2, 2 * EDGES_G], BF16)
        q_win = sb("q_win", [P, 4, C])
        dist = sb("dist", [P, 2, EDGES_G], BF16)
        hot_ne = sb("hot_ne", [P, 4, EDGES_G])
        dist_en = sb("dist_en", [P, 2, TILES_G, P], BF16)
        hot_en = sb("hot_en", [P, 4, TILES_G, P])
        kve = sb("kve", [P, 4, TILES_G, 2, C])
        prod = sb("prod", [P, 2, EDGES_G])
        logit = sb("logit", [P, TILES * H])
        top = sb("top", [P, 1])
        neg_pair = sb("neg_pair", [1, 1])
        neg_max = sb("neg_max", [1, 2])
        neg_max_b = sb("neg_max_b", [P, 2])
        fade = sb("fade", [P, 2])
        wv = sb("wv", [P, 4, TILES_G, AC])
        shift = sb("shift", [P, 2, P])
        sums = sb("sums", [P, 4, AC])

        g_kve = kve[:, 2, 0, :, :]
        g_kv = kv[:, 0, 0, :]
        g_q = kv[:, 0, 1, 0:C]
        g_ea = ea[:, 0, 0:P]
        g_prod = prod[:, 0, 0:C]
        g_dst = prod[:, 1, 0:P].bitcast(I32)
        g_dst_f = prod[:, 1, P:2 * P]
        g_same = hot_ne[:, 0, 0:P]
        g_apart = hot_ne[:, 0, P:2 * P]
        g_before = hot_ne[:, 0, 2 * P:3 * P]
        g_own = kve[:, 0, :, :, :].rearrange("p t a c -> p (t a) c")
        g_peers = kve[:, 1, :, :, :].rearrange("p t a c -> p (t a) c")
        g_wv = wv[:, 0, 0, :]
        g_old = sums[:, 0, :]
        g_new = sums[:, 1, :]
        g_low = kve[:, 3, :, :, :].rearrange("p t a c -> p (t a c)")[:, 0:BLOCKS * H]
        g_logit = sb("g_logit", [P, H])
        g_old_max = sb("g_old_max", [P, H])
        g_max = sb("g_max", [P, H])
        g_exp = sb("g_exp", [P, 2, H])
        g_node = sb("g_node", [P, 2])
        g_idx = sb("g_idx", [P, 2], I32)
        g_put = sb("g_put", [P, 1], I32)

        dst_rows = logit[0:PAIRS // 2, 0:2 * PAIR].bitcast(I32)
        dst_rows_f = logit[0:PAIRS // 2, 2 * PAIR:4 * PAIR]
        carve = [0]

        def part(*shape):
            size = 1
            for n in shape:
                size *= n
            view = logit[:, carve[0]:carve[0] + size]
            carve[0] += size
            if len(shape) == 1:
                return view
            names = ["a", "b", "c"][:len(shape)]
            return view.rearrange(f"p ({' '.join(names)}) -> p {' '.join(names)}", **dict(zip(names, shape)))

        n_sum = [part(FB, AC) for _ in range(2)]
        tab_flat = tab_buf[:, :, :, :].rearrange("p s b c -> p (s b c)")
        n_x = [tab_flat[:, k * FB * C:(k + 1) * FB * C].rearrange("p (b c) -> p b c", c=C) for k in range(2)]
        n_res = [part(FB, C) for _ in range(2)]
        n_xt = [tab_flat[:, 2 * FB * C:3 * FB * C],
                xt_buf[:, :, :].rearrange("p s c -> p (s c)")[:, 0:FB * P]]
        n_att = [part(FB, C) for _ in range(2)]
        n_skip = [part(FB, C + 1) for _ in range(2)]
        n_junk = part(FB * C).rearrange("p (k c) -> p k c", k=FB)
        n_rz = sb("n_rz", [P, 2, FB, H])
        n_gate = sb("n_gate", [P, 2, 3, FB])
        n_bn = sb("n_bn", [P, 2, FB, 6])
        n_mv = sb("n_mv", [P, 2, 2, FB, 2])
        n_var = sb("n_var", [P, 2, 2, FB])
        n_inv = sb("n_inv", [P, 2, 2, FB])
        n_off = sb("n_off", [P, 2, 2, FB])
        power = sb("power", [P, FB])

        kvq_ld = sem("kvq_ld")
        w_ld = sem("w_ld")
        ix_ld = sem("ix_ld")
        dst_ld = sem("dst_ld")
        iota_ok = sem("iota_ok")
        zeros_ok = sem("zeros_ok")
        ident_ok = sem("ident_ok")
        row_cast = sem("row_cast")
        gate_ok = sem("gate_ok")
        bq_ok = sem("bq_ok")
        w_ok = sem("w_ok")
        xt_ld = [sem(f"xt_ld{s}") for s in range(TSLOTS)]
        tab_mm = sem("tab_mm")
        tab_ev = sem("tab_ev")
        tab_st = [sem(f"tab_st{s}") for s in range(TSLOTS)]
        zero_st = sem("zero_st")
        setup = sem("setup")
        first_mm = sem("first_mm")
        rel_st = sem("rel_st")
        bad_ok = sem("bad_ok")
        flag_ok = sem("flag_ok")
        low_ok = sem("low_ok")
        lows_ok = sem("lows_ok")
        wide_steps = sem("wide_steps")
        spread_ok = sem("spread_ok")
        wide_ok = sem("wide_ok")

        ea_ld = [sem(f"ea_ld{p}") for p in range(2)]
        row_ld = [sem(f"row_ld{p}") for p in range(2)]
        qw_ld = [sem(f"qw_ld{p}") for p in range(2)]
        kv_ld = [sem(f"kv_ld{s}") for s in range(4)]
        idx_ok = sem("idx_ok")
        row_ok = sem("row_ok")
        e_ok = sem("e_ok")
        q_ok = sem("q_ok")
        topT_ok = sem("topT_ok")
        maxb_ok = sem("maxb_ok")
        sum_ok = sem("sum_ok")
        dist_ok = sem("dist_ok")
        hotne_ok = sem("hotne_ok")
        disten_ok = sem("disten_ok")
        negm_ok = sem("negm_ok")
        fade_ok = sem("fade_ok")
        exp_ok = sem("exp_ok")
        sums_ok = sem("sums_ok")
        kve_ok = sem("kve_ok")
        prod_ok = sem("prod_ok")
        logit_ok = sem("logit_ok")
        top_ok = sem("top_ok")
        negp_ok = sem("negp_ok")
        max_ok = sem("max_ok")
        hoten_ok = sem("hoten_ok")
        wv_ok = sem("wv_ok")
        shift_ok = sem("shift_ok")
        sums_st = sem("sums_st")

        n_ld = [sem(f"n_ld{p}") for p in range(2)]
        x_ld = [sem(f"x_ld{p}") for p in range(2)]
        nxt_ld = [sem(f"nxt_ld{p}") for p in range(2)]
        g_low_ok = sem("g_low_ok")
        g_init = sem("g_init")
        g_io = [sem(f"g_io{k}") for k in range(2)]
        g_ld = sem("g_ld")
        g_idx_ok = sem("g_idx_ok")
        g_get = [sem(f"g_get{k}") for k in range(4)]
        g_go = sem("g_go")
        g_pe = sem("g_pe")
        g_dve = sem("g_dve")
        g_act = sem("g_act")
        slot_free = sem("slot_free")
        store_free = sem("store_free")
        stats_in = sem("stats_in")
        n_mm = sem("n_mm")
        z_ok = sem("z_ok")
        rz_ok = sem("rz_ok")
        att_ok = sem("att_ok")
        skip_ok = sem("skip_ok")
        diff_ok = sem("diff_ok")
        score_ok = sem("score_ok")
        total_ok = sem("total_ok")
        gexp_ok = sem("gexp_ok")
        gden_ok = sem("gden_ok")
        gate_done = sem("gate_done")
        mix_ok = sem("mix_ok")
        bn_ok = [sem(f"bn_ok{k}") for k in range(2)]
        mv_ok = [sem(f"mv_ok{k}") for k in range(2)]
        var_ok = [sem(f"var_ok{k}") for k in range(2)]
        inv_ok = [sem(f"inv_ok{k}") for k in range(2)]
        off_ok = [sem(f"off_ok{k}") for k in range(2)]
        norm_ok = [sem(f"norm_ok{k}") for k in range(2)]
        gamma_ok = sem("gamma_ok")
        beta_ok = sem("beta_ok")
        twice_ok = sem("twice_ok")
        res_ok = sem("res_ok")
        power_ok = sem("power_ok")
        wskip_ok = sem("wskip_ok")
        n_out = [sem(f"n_out{p}") for p in range(2)]

        block = ctx.enter_context(nc.Block())

        kv_rows = kv_tab.rearrange("(b p) c -> p b c", p=P)
        q_rows = q_tab.rearrange("(b p) c -> p b c", p=P)
        sum_rows = sum_tab.rearrange("(b p) c -> p b c", p=P)
        x_rows = x.rearrange("(b p) c -> p b c", p=P)
        out_rows = out.rearrange("(b p) c -> p b c", p=P)
        dst_line = dst.rearrange("(one e) -> one e", one=1)
        sum_zero = sum_tab.rearrange("(p j) c -> p (j c)", p=P)

        tab_rounds = BLOCKS // TB // TSLOTS
        rounds = PAIRS // ROUND
        assert rounds * ROUND == PAIRS and tab_rounds * TSLOTS * TB == BLOCKS
        tab_banks = [e_ps[0], e_ps[1], q_ps[0]]
        skip_banks = tab_banks
        G_OWN, G_EXP, G_WV, G_DVE = 4, 18, 20, 23
        batches = OUT_BLOCKS // FB

        @block.sync
        def _(sp):
            for k, name in enumerate(("Wk", "Wv", "Wq")):
                sp.dma_start(w_kvq[:, k * C:(k + 1) * C], w[name]).then_inc(kvq_ld, 16)
            for k, name in enumerate(("bk", "bv", "bq")):
                sp.dma_start(b_kvq[:, k * C:(k + 1) * C], w[name].partition_broadcast(P)).then_inc(kvq_ld, 16)

            def table_load(i, j):
                sp.dma_start(xt_buf[:, j, :], xT[:, bass.ds((i * TSLOTS + j) * (TB * P), TB * P)]
                             ).then_inc(xt_ld[j], 16)

            def table_store(i, j):
                sp.wait_ge(tab_ev, (i * TSLOTS + j + 1) * TB)
                rows = bass.ds((i * TSLOTS + j) * TB, TB)
                sp.dma_start(kv_rows[:, rows, :], tab_buf[:, j, :, 0:2 * C]).then_inc(tab_st[j], 16)
                sp.dma_start(q_rows[:, rows, :], tab_buf[:, j, :, 2 * C:3 * C]).then_inc(tab_st[j], 16)

            for j in range(TSLOTS):
                table_load(0, j)
            sp.dma_start(dst_all[:, :], dstT).then_inc(dst_ld, 16)
            sp.dma_start(dst_rows, dst.rearrange("(p j) -> p j", j=2 * PAIR)).then_inc(dst_ld, 16)
            sp.dma_start(src_all[:, :], srcT).then_inc(ix_ld, 16)
            sp.dma_start(we[:, :], w["We"]).then_inc(w_ld, 16)
            sp.dma_start(wskip[:, 0:C], w["Wskip"]).then_inc(w_ld, 16)
            for t, name in ((bskip, "bskip"), (gamma, "ln_gamma"), (beta_ln, "ln_beta")):
                sp.dma_start(t[:, :], w[name].partition_broadcast(P)).then_inc(w_ld, 16)
            sp.dma_start(wbeta[:, :, :].rearrange("p a c -> p (a c)"), w["Wbeta"].partition_broadcast(P)
                         ).then_inc(w_ld, 16)
            with sp.Fori(0, tab_rounds - 1) as i:
                for j in range(TSLOTS):
                    table_store(i, j)
                    table_load(i + 1, j)
            for j in range(TSLOTS):
                table_store(tab_rounds - 1, j)
            sp.wait_ge(row_cast, 1)
            sp.dma_start(rel_row.rearrange("one (p j) -> (one p) j", j=2 * PAIR), rel_rows[:, :]
                         ).then_inc(rel_st, 16)
            for j in range(TSLOTS):
                sp.wait_ge(tab_st[j], 32 * tab_rounds)
            sp.wait_ge(rel_st, 16)
            sp.wait_ge(flag_ok, 1)
            grouped = sp.value_load(flag[0:1, 0:1], min_val=0, max_val=1)

            def load_x(b, p):
                sp.dma_start(n_x[p], x_rows[:, bass.ds(b * FB, FB), :]).then_inc(x_ld[p], 16)

            def load_xt(b, p):
                sp.dma_start(n_xt[p], xT[:, bass.ds(b * (FB * P), FB * P)]).then_inc(nxt_ld[p], 16)

            def first_x():
                for p in range(2):
                    load_xt(p, p)
                    load_x(p, p)

            def window(g):
                return sp.value_load(dst_all[0:1, bass.ds(g * TILES_G, 1)], min_val=0, max_val=N_NODES)

            def load(q, par, reuse):
                if reuse:
                    sp.wait_ge(e_ok, 2 * q - 2)
                    sp.wait_ge(row_ok, 2 * q - 2)
                    sp.wait_ge(q_ok, 2 * q - 2)
                sp.dma_start(ea[:, par, :], eaT[:, bass.ds(q * PAIR, PAIR)]).then_inc(ea_ld[par], 16)
                sp.dma_start(row[:, par, :], rel_row[:, bass.ds(q * PAIR, PAIR)]).then_inc(row_ld[par], 16)
                for u in range(2):
                    sp.dma_start(q_win[:, 2 * par + u, :], q_tab[bass.ds(window(2 * q + u), P), :]
                                 ).then_inc(qw_ld[par], 16)

            def store(q, par, ordered=(True, True)):
                for u in range(2):
                    g = 2 * q + u
                    w0 = window(g)
                    if not ordered[u]:
                        sp.wait_ge(sums_ok, g + 2)
                    else:
                        sp.wait_ge(sums_st, 16 * g)
                        sp.sem_inc(store_free, 1)
                        sp.wait_ge(sums_ok, g + 2)
                        sp.sem_inc(store_free, 1)
                    sp.dma_start(sum_tab[bass.ds(w0, P), :], sums[:, 2 * par + u, :]).then_inc(sums_st, 16)

            with sp.If(grouped):
                def zero_sums(first, end):
                    for k in range(first, end):
                        sp.dma_start(sum_zero[:, k * ZERO_W:(k + 1) * ZERO_W], zeros[:, :]).then_inc(zero_st, 16)

                load(0, 0, False)
                load(1, 1, False)
                sp.wait_ge(zeros_ok, 1)
                zero_sums(0, ZERO_DMAS // 2)
                load(2, 0, True)
                zero_sums(ZERO_DMAS // 2, ZERO_DMAS)
                load(3, 1, True)
                sp.wait_ge(zero_st, 16 * ZERO_DMAS)
                store(0, 0, (False, True))
                load(4, 0, True)
                store(1, 1)
                load(5, 1, True)
                store(2, 0)
                load(6, 0, True)
                store(3, 1)
                load(7, 1, True)
                store(4, 0)
                with sp.Fori(2, rounds) as i:
                    for k in range(ROUND):
                        load(ROUND * i + k, k % 2, True)
                        store(ROUND * i + k - 3, (k + 1) % 2)
                first_x()
                for q in range(PAIRS - 3, PAIRS):
                    store(q, q % 2)
                sp.wait_ge(sums_st, 16 * GROUPS)
            with sp.Else():
                first_x()
            sp.wait_ge(wide_ok, 1)
            general = sp.value_load(wide[0:1, 0:1], min_val=0, max_val=1)
            with sp.If(general):
                for k in range(ZERO_DMAS):
                    sp.dma_start(sum_zero[:, k * ZERO_W:(k + 1) * ZERO_W], zeros[:, :]).then_inc(g_init, 16)
                sp.wait_ge(g_low_ok, 1)
                sp.dma_start(max_tab.rearrange("(p j) h -> p (j h)", p=P), g_low).then_inc(g_init, 16)

                def tile_load(t):
                    sp.dma_start(g_ea, eaT[:, bass.ds(t * P, P)]).then_inc(g_ld, 16)
                    sp.dma_start(g_dst, dst_line[:, bass.ds(t * P, P)].to_broadcast([P, P])).then_inc(g_ld, 16)

                tile_load(0)
                with sp.Fori(1, TILES) as t:
                    for k in range(2):
                        sp.wait_ge(g_io[k], 16 * t)
                    tile_load(t)
                sp.wait_ge(g_init, 16 * (ZERO_DMAS + 1))
                for k in range(2):
                    sp.wait_ge(g_io[k], 16 * TILES)

            def load_sums(b, p):
                sp.dma_start(n_sum[p], sum_rows[:, bass.ds(b * FB, FB), :]).then_inc(n_ld[p], 16)

            def node_store(b, p):
                sp.wait_ge(norm_ok[1], b + 1)
                sp.dma_start(out_rows[:, bass.ds(b * FB, FB), :], n_res[p]).then_inc(n_out[p], 16)

            def node_step(b, p, store=True, x=True, sums_too=True):
                if store:
                    node_store(b - 2, p)
                if x:
                    sp.wait_ge(res_ok, b)
                    load_x(b + 1, 1 - p)
                if sums_too:
                    sp.wait_ge(att_ok, b + 2)
                    load_sums(b + 3, 1 - p)
                    sp.wait_ge(n_mm, b + 2)
                    load_xt(b + 3, 1 - p)

            load_sums(0, 0)
            load_sums(1, 1)
            sp.wait_ge(n_mm, 1)
            load_xt(2, 0)
            sp.wait_ge(att_ok, 1)
            load_sums(2, 0)
            node_step(0, 0, store=False, x=False)
            node_step(1, 1, store=False)
            with sp.Fori(1, batches // 2 - 2) as i:
                node_step(2 * i, 0)
                node_step(2 * i + 1, 1)
            node_step(batches - 4, 0)
            node_step(batches - 3, 1, sums_too=False)
            node_step(batches - 2, 0, sums_too=False)
            node_step(batches - 1, 1, x=False, sums_too=False)
            node_store(batches - 2, 0)
            node_store(batches - 1, 1)
            for p in range(2):
                sp.wait_ge(n_out[p], 16 * (batches // 2))

        @block.gpsimd
        def _(pool):
            pool.memset(zeros[:, :], 0.0).then_inc(zeros_ok, 1)
            pool.iota(iota_pn[:, :], [[-1, P]], base=0, channel_multiplier=1,
                      allow_small_or_imprecise_dtypes=True).then_inc(iota_ok, 1)
            pool.iota(iota_n[:, :], [[1, P]], base=0, channel_multiplier=0,
                      allow_small_or_imprecise_dtypes=True).then_inc(iota_ok, 1)
            pool.iota(neg_p[:, :], [[0, 1]], base=0, channel_multiplier=-1,
                      allow_small_or_imprecise_dtypes=True).then_inc(iota_ok, 1)
            pool.wait_ge(setup, 9)
            pool.partition_all_reduce(bad_all[:, :], bad[:, 3:4], P, RMAX).then_inc(bad_ok, 1)
            pool.wait_ge(flag_ok, 1)
            grouped = pool.value_load(flag[0:1, 0:1], min_val=0, max_val=1)
            for j in range(TSLOTS):
                pool.wait_ge(tab_st[j], 32 * tab_rounds)

            def gather(q, par, reuse):
                for u in range(2):
                    s = 2 * par + u
                    if reuse:
                        pool.wait_ge(kve_ok, 2 * q + u - 3)
                    else:
                        pool.wait_ge(idx_ok, q + 1)
                    pool.sem_inc(slot_free, 1)
                    for t in range(TILES_G):
                        pool.indirect_dma_start(
                            out=kv[:, s, t, :], out_offset=None, in_=kv_tab[:, :],
                            in_offset=bass.IndirectOffsetOnAxis(
                                ap=idx[:, par, u * TILES_G + t:u * TILES_G + t + 1], axis=0),
                        ).then_inc(kv_ld[s], 16)

            with pool.If(grouped):
                gather(0, 0, False)
                gather(1, 1, False)
                gather(2, 0, True)
                gather(3, 1, True)
                with pool.Fori(1, rounds) as i:
                    for k in range(ROUND):
                        gather(ROUND * i + k, k % 2, True)
            pool.wait_ge(wide_steps, 2)
            pool.partition_all_reduce(spread[:, 2:4], spread[:, 0:2], P, RMAX).then_inc(spread_ok, 1)
            pool.wait_ge(wide_ok, 1)
            general = pool.value_load(wide[0:1, 0:1], min_val=0, max_val=1)
            with pool.If(general):

                def tile_rows(t):
                    pool.sem_inc(g_go, 1)
                    pool.tensor_copy(g_idx[:, 0:1], src_all[:, bass.ds(t, 1)]).then_inc(g_idx_ok, 1)
                    pool.tensor_copy(g_idx[:, 1:2], dst_all[:, bass.ds(t, 1)]).then_inc(g_idx_ok, 1)
                    pool.wait_ge(g_idx_ok, 2 * t + 2)
                    pool.sem_inc(g_go, 1)
                    for k, (to, table, col) in enumerate(((g_kv, kv_tab, 0), (g_q, q_tab, 1), (g_old, sum_tab, 1),
                                                          (g_old_max[:, :], max_tab, 1))):
                        pool.indirect_dma_start(
                            out=to, out_offset=None, in_=table[:, :],
                            in_offset=bass.IndirectOffsetOnAxis(ap=g_idx[:, col:col + 1], axis=0),
                        ).then_inc(g_get[k], 16)
                    pool.wait_ge(g_dve, G_DVE * (t + 1))
                    pool.sem_inc(g_go, 1)
                    for k, (table, of) in enumerate(((sum_tab, g_new), (max_tab, g_max[:, :]))):
                        pool.indirect_dma_start(
                            out=table[:, :], out_offset=bass.IndirectOffsetOnAxis(ap=g_put[:, :], axis=0),
                            in_=of, in_offset=None, bounds_check=ROWS - 1, oob_is_err=False,
                        ).then_inc(g_io[k], 16)

                pool.wait_ge(ix_ld, 16)
                pool.wait_ge(g_init, 16 * (ZERO_DMAS + 1))
                tile_rows(0)
                with pool.Fori(1, TILES) as t:
                    for k in range(2):
                        pool.wait_ge(g_io[k], 16 * t)
                    tile_rows(t)

            pool.memset(power[:, :], -0.5).then_inc(power_ok, 1)
            pool.wait_ge(power_ok, 1)
            pool.wait_ge(w_ld, 16 * W_DMAS)

            def deviation(b, p, k):
                pool.wait_ge(mv_ok[k], b + 1)
                pool.sem_inc(power_ok, 1)
                pool.tensor_scalar(n_var[:, p, k, :], n_mv[:, p, k, :, 1], EPS, None, ALU.add).then_inc(var_ok[k], 1)
                pool.wait_ge(var_ok[k], b + 1)
                pool.tensor_tensor(n_inv[:, p, k, :], n_var[:, p, k, :], power[:, :], ALU.pow).then_inc(inv_ok[k], 1)

            def difference(b, p):
                pool.wait_ge(skip_ok, b + 1)
                pool.wait_ge(att_ok, b + 1)
                pool.tensor_tensor(n_skip[p][:, :, 0:C], n_skip[p][:, :, 0:C], n_att[p], ALU.subtract
                                   ).then_inc(diff_ok, 1)

            def scale(b, p):
                pool.wait_ge(norm_ok[0], b + 1)
                pool.tensor_tensor(n_att[p], n_att[p], gamma[:, :].unsqueeze(1).to_broadcast([P, FB, C]), ALU.mult
                                   ).then_inc(gamma_ok, 1)

            def centre(b, p):
                pool.wait_ge(gamma_ok, b + 1)
                pool.tensor_tensor(n_att[p], n_att[p], beta_ln[:, :].unsqueeze(1).to_broadcast([P, FB, C]), ALU.add
                                   ).then_inc(beta_ok, 1)

            def node_step(b, p, before=2, after=True):
                if before:
                    scale(b - 1, 1 - p)
                if before == 2:
                    deviation(b - 2, p, 1)
                if before:
                    centre(b - 1, 1 - p)
                deviation(b, p, 0)
                if after:
                    difference(b + 1, 1 - p)

            difference(0, 0)
            node_step(0, 0, before=0)
            node_step(1, 1, before=1)
            with pool.Fori(1, batches // 2 - 1) as i:
                node_step(2 * i, 0)
                node_step(2 * i + 1, 1)
            node_step(batches - 2, 0)
            node_step(batches - 1, 1, after=False)
            scale(batches - 1, 1)
            deviation(batches - 2, 0, 1)
            centre(batches - 1, 1)
            deviation(batches - 1, 1, 1)

        @block.tensor
        def _(pe):
            pe.wait_ge(w_ok, 1)

            def table_step(i, j, reuse):
                pe.wait_ge(xt_ld[j], 16 * (i + 1))
                for b in range(TB):
                    if reuse:
                        pe.wait_ge(tab_ev, (i * TSLOTS + j - 1) * TB + b + 1)
                    pe.matmul(tab_banks[b][:, 0:3 * C], xt_buf[:, j, b * P:(b + 1) * P], w_kvq[:, :],
                              start=True, stop=True).then_inc(tab_mm, 1)

            for j in range(TSLOTS):
                table_step(0, j, j > 0)
            pe.wait_ge(setup, 2)
            pe.matmul(max_ps[:, 0:GROUPS], ones_f[:, :], first[:, :], start=True, stop=True).then_inc(first_mm, 1)
            with pe.Fori(1, tab_rounds) as i:
                for j in range(TSLOTS):
                    table_step(i, j, True)
            pe.wait_ge(flag_ok, 1)
            grouped = pe.value_load(flag[0:1, 0:1], min_val=0, max_val=1)
            pe.wait_ge(tab_ev, BLOCKS)
            pe.wait_ge(w_ld, 16 * W_DMAS)

            def spread_row(q, par, u, i, first_use=False):
                g = 2 * q + u
                if u == 0:
                    pe.wait_ge(row_ld[par], 16 * (i + 1))
                if not (first_use and par == 0 and u == 0):
                    pe.wait_ge(dist_ok, g)
                pe.matmul(row_ps[:, :], ones_b[:, :], row[:, par, u * EDGES_G:(u + 1) * EDGES_G],
                          start=True, stop=True).then_inc(row_ok, 1)

            def edge_part(q, par, u, i, first_use):
                g = 2 * q + u
                if u == 0:
                    pe.wait_ge(ea_ld[par], 16 * (i + 1))
                if not first_use:
                    pe.wait_ge(kve_ok, g - 1)
                for t in range(TILES_G):
                    mm = pe.matmul(e_ps[u][:, t * P:(t + 1) * P],
                                   ea[:, par, (u * TILES_G + t) * P:(u * TILES_G + t + 1) * P], we[:, :],
                                   start=True, stop=True)
                mm.then_inc(e_ok, 1)

            def q_spread(q, par, u, i, first_use):
                g = 2 * q + u
                if u == 0:
                    pe.wait_ge(qw_ld[par], 32 * (i + 1))
                pe.wait_ge(hotne_ok, g + 1)
                if not (first_use and par == 0):
                    pe.wait_ge(prod_ok, g - 1)
                for t in range(TILES_G):
                    mm = pe.matmul(q_ps[u][:, t * P:(t + 1) * P], hot_ne[:, 2 * par + u, t * P:(t + 1) * P],
                                   q_win[:, 2 * par + u, :], start=True, stop=True)
                mm.then_inc(q_ok, 1)

            def top_row(q, first_use=False):
                pe.wait_ge(top_ok, q + 1)
                if not first_use:
                    pe.wait_ge(negp_ok, q)
                pe.transpose(max_ps[0:1, 0:P], top[:, :], ident[:, :]).then_inc(topT_ok, 1)

            def max_spread(q, first_use=False):
                pe.wait_ge(max_ok, q + 2)
                if not first_use:
                    pe.wait_ge(negm_ok, q)
                pe.matmul(max_ps[:, 256:258], ones_f[:, :], neg_max[:, :], start=True, stop=True).then_inc(maxb_ok, 1)

            def node_sums(q, par, u, first_use=False):
                g = 2 * q + u
                s = 2 * par + u
                pe.wait_ge(hoten_ok, g + 1)
                pe.wait_ge(wv_ok, g + 1)
                if not first_use:
                    pe.wait_ge(sums_ok, g)
                for t in range(TILES_G):
                    pe.matmul(sum_ps[u][:, 0:AC], hot_en[:, s, t, :], wv[:, s, t, :], start=(t == 0), stop=False)
                pe.wait_ge(shift_ok, g + 1)
                pe.wait_ge(sums_ok, g + 1)
                pe.matmul(sum_ps[u][:, 0:AC], shift[:, u, :], sums[:, (s + 3) % 4, :],
                          start=False, stop=True).then_inc(sum_ok, 1)

            def step(q, par, i, first_use=False, last=False):
                before = not (first_use and par == 0)
                if before:
                    max_spread(q - 1, first_use)
                q_spread(q, par, 0, i, first_use)
                q_spread(q, par, 1, i, first_use)
                if not last:
                    spread_row(q + 1, 1 - par, 0, i + par)
                if before:
                    node_sums(q - 1, 1 - par, 0, first_use)
                if not last:
                    spread_row(q + 1, 1 - par, 1, i + par)
                    edge_part(q + 1, 1 - par, 0, i + par, False)
                if before:
                    node_sums(q - 1, 1 - par, 1, first_use)
                top_row(q, not before)
                if not last:
                    edge_part(q + 1, 1 - par, 1, i + par, False)

            with pe.If(grouped):
                for u in range(2):
                    spread_row(0, 0, u, 0, True)
                    edge_part(0, 0, u, 0, True)
                step(0, 0, 0, True)
                step(1, 1, 0, True)
                step(2, 0, 1)
                step(3, 1, 1)
                with pe.Fori(1, rounds - 1) as i:
                    for k in range(ROUND):
                        step(ROUND * i + k, k % 2, (ROUND // 2) * i + k // 2)
                for q in range(PAIRS - ROUND, PAIRS):
                    step(q, q % 2, q // 2, last=q == PAIRS - 1)
                max_spread(PAIRS - 1)
                node_sums(PAIRS - 1, 1, 0)
                node_sums(PAIRS - 1, 1, 1)

            pe.wait_ge(wide_ok, 1)
            general = pe.value_load(wide[0:1, 0:1], min_val=0, max_val=1)
            with pe.If(general):
                with pe.Fori(0, TILES) as t:
                    pe.wait_ge(g_ld, 32 * t + 32)
                    pe.matmul(e_ps[0][:, 0:C], g_ea, we[:, :], start=True, stop=True).then_inc(g_pe, 1)
                    pe.wait_ge(g_dve, G_DVE * t + G_OWN)
                    for h in range(H):
                        mm = pe.matmul(q_ps[h // 4][:, (h % 4) * P:(h % 4 + 1) * P], g_own[:, h, :], ident[:, :],
                                       start=True, stop=True)
                    mm.then_inc(g_pe, 1)
                    pe.wait_ge(g_dve, G_DVE * t + G_WV)
                    pe.matmul(sum_ps[0][:, 0:AC], g_same, g_wv, start=True, stop=True).then_inc(g_pe, 1)

            pe.wait_ge(wskip_ok, 2)

            def skip_project(b, p, i, reuse):
                pe.wait_ge(nxt_ld[p], 16 * (i + 1))
                if reuse:
                    pe.wait_ge(skip_ok, b)
                for k in range(FB):
                    to = skip_banks[k // 3][:, (k % 3) * (C + 1):(k % 3 + 1) * (C + 1)]
                    pe.matmul(to, n_xt[p][:, k * P:(k + 1) * P], wskip[:, :], start=True, stop=False)
                    mm = pe.matmul(to, ones_f[:, :], skip_row[:, :], start=False, stop=True)
                mm.then_inc(n_mm, 1)

            skip_project(0, 0, 0, False)
            skip_project(1, 1, 0, True)
            with pe.Fori(1, batches // 2) as i:
                skip_project(2 * i, 0, i, True)
                skip_project(2 * i + 1, 1, i, True)

        @block.scalar
        def _(act):
            act.wait_ge(flag_ok, 1)
            grouped = act.value_load(flag[0:1, 0:1], min_val=0, max_val=1)
            act.wait_ge(iota_ok, 3)
            act.wait_ge(setup, 7)

            def distance(q, par, u, first_use=False):
                g = 2 * q + u
                act.wait_ge(row_ok, g + 1)
                if not (first_use and par == 0):
                    act.wait_ge(hotne_ok, g - 1)
                act.activation(dist[:, u, :], row_ps[:, :], ACT.Abs, bias=neg_p[:, :]).then_inc(dist_ok, 1)

            def one_hot(q, par, u, reuse):
                g = 2 * q + u
                act.wait_ge(dist_ok, g + 1)
                if reuse:
                    act.wait_ge(q_ok, g - 3)
                act.activation(hot_ne[:, 2 * par + u, :], dist[:, u, :], ACT.Relu, bias=1.0, scale=-1.0
                               ).then_inc(hotne_ok, 1)

            def edge_distance(q, u, first_use=False):
                g = 2 * q + u
                if not first_use:
                    act.wait_ge(hoten_ok, g - 1)
                for t in range(TILES_G):
                    last = act.activation(dist_en[:, u, t, :], iota_n[:, :], ACT.Abs,
                                          bias=neg_rel[:, bass.ds(g * TILES_G + t, 1)])
                last.then_inc(disten_ok, 1)

            def edge_one_hot(q, par, u, reuse):
                g = 2 * q + u
                act.wait_ge(disten_ok, g + 1)
                if reuse:
                    act.wait_ge(sum_ok, g - 3)
                act.activation(hot_en[:, 2 * par + u, :, :], dist_en[:, u, :, :], ACT.Relu, bias=1.0, scale=-1.0
                               ).then_inc(hoten_ok, 1)

            def maximum_out(q, first_use=False):
                act.wait_ge(maxb_ok, q + 1)
                if not first_use:
                    act.wait_ge(exp_ok, q)
                    act.wait_ge(fade_ok, q)
                act.copy(neg_max_b[:, :], max_ps[:, 256:258]).then_inc(negm_ok, 1)

            def weights(q, par):
                act.wait_ge(negm_ok, q + 1)
                act.wait_ge(logit_ok, 2 * q + 2)
                if reused[0]:
                    act.wait_ge(sum_ok, 2 * q - 2)
                act.activation(wv[:, 2 * par:2 * par + 2, :, C:AC].rearrange("p a t h -> p (a t) h"),
                               logit[:, bass.ds(q * (TILES_Q * H), TILES_Q * H)].rearrange("p (t h) -> p t h", h=H),
                               ACT.Exp, bias=neg_max_b[:, par:par + 1]).then_inc(exp_ok, 1)
                if reused[0]:
                    act.wait_ge(shift_ok, 2 * q - 3)
                act.activation(fade[:, par:par + 1], neg_max_b[:, 1 - par:2 - par], ACT.Exp, scale=-1.0,
                               bias=neg_max_b[:, par:par + 1]).then_inc(fade_ok, 1)

            def sums_out(q, par, u):
                g = 2 * q + u
                act.wait_ge(sum_ok, g + 1)
                if reused[0]:
                    act.wait_ge(sums_st, 16 * (g - 3))
                act.copy(sums[:, 2 * par + u, :], sum_ps[u][:, 0:AC]).then_inc(sums_ok, 1)

            reused = [False]

            def step(q, par, reuse=True, first_use=False, last=False):
                before = not (first_use and par == 0)
                if before:
                    weights(q - 1, 1 - par)
                edge_distance(q, 0, first_use and par == 0)
                if not last:
                    distance(q + 1, 1 - par, 0)
                edge_one_hot(q, par, 0, reuse)
                if not last:
                    one_hot(q + 1, 1 - par, 0, reuse or par == 1)
                if before:
                    sums_out(q - 1, 1 - par, 0)
                if not last:
                    distance(q + 1, 1 - par, 1)
                    one_hot(q + 1, 1 - par, 1, reuse or par == 1)
                if before:
                    sums_out(q - 1, 1 - par, 1)
                edge_distance(q, 1, first_use and par == 0)
                maximum_out(q, first_use and par == 0)
                edge_one_hot(q, par, 1, reuse)

            with act.If(grouped):
                for u in range(2):
                    distance(0, 0, u, True)
                    one_hot(0, 0, u, False)
                step(0, 0, False, True)
                step(1, 1, False, True)
                step(2, 0)
                reused[0] = True
                step(3, 1)
                with act.Fori(1, rounds - 1) as i:
                    for k in range(ROUND):
                        step(ROUND * i + k, k % 2)
                for q in range(PAIRS - ROUND, PAIRS):
                    step(q, q % 2, last=q == PAIRS - 1)
                weights(PAIRS - 1, 1)
                sums_out(PAIRS - 1, 1, 0)
                sums_out(PAIRS - 1, 1, 1)

            act.wait_ge(wide_ok, 1)
            general = act.value_load(wide[0:1, 0:1], min_val=0, max_val=1)
            with act.If(general):
                with act.Fori(0, TILES) as t:
                    act.wait_ge(g_dve, G_DVE * t + G_EXP)
                    act.activation(g_exp[:, :, :], g_exp[:, :, :], ACT.Exp).then_inc(g_act, 1)

            def skip_out(b, p, reuse=True):
                act.wait_ge(n_mm, b + 1)
                if reuse:
                    act.wait_ge(mix_ok, b - 1)
                for k in range(0, FB, 3):
                    n = min(3, FB - k)
                    last = act.copy(n_skip[p][:, k:k + n, :],
                                    skip_banks[k // 3][:, 0:n * (C + 1)].rearrange("p (k c) -> p k c", c=C + 1))
                last.then_inc(skip_ok, 1)

            def gate_exp(b, p):
                act.wait_ge(total_ok, b + 1)
                act.activation(n_gate[:, p, 2, :], n_gate[:, p, 1, :], ACT.Exp, scale=-1.0).then_inc(gexp_ok, 1)

            def twice_x(p, i):
                act.wait_ge(x_ld[p], 16 * (i + 1))
                act.mul(n_x[p], n_x[p], 2.0).then_inc(twice_ok, 1)

            def norm(b, p, k, rows):
                act.wait_ge(off_ok[k], b + 1)
                for j in range(FB):
                    last = act.activation(rows[p][:, j, :], rows[p][:, j, :], ACT.Identity,
                                          bias=n_off[:, p, k, j:j + 1], scale=n_inv[:, p, k, j:j + 1])
                last.then_inc(norm_ok[k], 1)

            def node_step(b, p, i, before=True, reuse=True, after=True):
                if before:
                    norm(b - 2, p, 1, n_res)
                if after:
                    skip_out(b + 1, 1 - p, reuse)
                norm(b, p, 0, n_att)
                if after:
                    gate_exp(b + 1, 1 - p)
                twice_x(p, i)

            skip_out(0, 0, False)
            gate_exp(0, 0)
            node_step(0, 0, 0, before=False, reuse=False)
            node_step(1, 1, 0, before=False)
            with act.Fori(1, batches // 2 - 1) as i:
                node_step(2 * i, 0, i)
                node_step(2 * i + 1, 1, i)
            node_step(batches - 2, 0, batches // 2 - 1)
            node_step(batches - 1, 1, batches // 2 - 1, after=False)
            norm(batches - 2, 0, 1, n_res)
            norm(batches - 1, 1, 1, n_res)

        @block.vector
        def _(dve):
            dve.memset(ones_f[:, :], 1.0)
            dve.memset(ones_b[:, :], 1.0)
            dve.memset(one_col[:, :], 1.0)
            dve.memset(neg_max[:, :], BIG).then_inc(max_ok, 1)
            dve.memset(sums[:, :, :], 0.0).then_inc(sums_ok, 1)
            dve.wait_ge(iota_ok, 2)
            dve.tensor_scalar(ident[:, :], iota_pn[:, :], 0.0, None, ALU.is_equal).then_inc(ident_ok, 1)
            dve.wait_ge(kvq_ld, 16 * KVQ_DMAS)
            dve.tensor_scalar(w_kvq[:, 2 * C:3 * C], w_kvq[:, 2 * C:3 * C], D ** -0.5, None, ALU.mult).then_inc(w_ok, 1)
            dve.tensor_scalar(b_kvq[:, 2 * C:3 * C], b_kvq[:, 2 * C:3 * C], D ** -0.5, None, ALU.mult).then_inc(bq_ok, 1)
            dve.wait_ge(bq_ok, 1)

            def table_round(i, reuse=True):
                for j in range(TSLOTS):
                    if reuse:
                        dve.wait_ge(tab_st[j], 32 * i)
                    for b in range(TB):
                        dve.wait_ge(tab_mm, (i * TSLOTS + j) * TB + b + 1)
                        dve.tensor_tensor(tab_buf[:, j, b, :], tab_banks[b][:, 0:3 * C], b_kvq[:, :],
                                          ALU.add).then_inc(tab_ev, 1)

            table_round(0, False)
            dve.wait_ge(dst_ld, 32)
            dve.tensor_copy(first[:, :], dst_all[0:1, 0:TILES:TILES_G]).then_inc(setup, 1)
            dve.tensor_copy(dst_rows_f, dst_rows).then_inc(setup, 1)
            dve.tensor_copy(neg_rel[:, :], dst_all[:, :]).then_inc(setup, 1)
            table_round(1)
            dve.wait_ge(first_mm, 1)
            dve.tensor_copy(first_b[:, :], max_ps[:, 0:GROUPS]).then_inc(setup, 1)
            dve.wait_ge(setup, 4)
            rows4 = dst_rows_f.rearrange("p (g e) -> p g e", e=EDGES_G)
            dve.tensor_tensor(rel_rows[:, :].rearrange("p (g e) -> p g e", e=EDGES_G), rows4,
                              rows4[:, :, 0:1].to_broadcast([PAIRS // 2, 4, EDGES_G]),
                              ALU.subtract).then_inc(row_cast, 1)
            table_round(2)
            rel3 = neg_rel[:, :].rearrange("p (g t) -> p g t", t=TILES_G)
            dve.tensor_tensor(rel3, first_b[:, :].unsqueeze(2).to_broadcast([P, GROUPS, TILES_G]), rel3,
                              ALU.subtract).then_inc(setup, 1)
            dve.memset(delta[:, 0:1], 0.0).then_inc(setup, 1)
            dve.tensor_tensor(delta[:, 1:GROUPS], first_b[:, 1:GROUPS], first_b[:, 0:GROUPS - 1],
                              ALU.subtract).then_inc(setup, 1)
            table_round(3)
            dve.wait_ge(setup, 7)
            dve.tensor_reduce(bad[:, 0:1], neg_rel[:, :], AX_X, ALU.max).then_inc(low_ok, 1)
            dve.tensor_reduce(bad[:, 2:3], delta[:, :], AX_X, ALU.min, negate=True).then_inc(low_ok, 1)
            table_round(4)
            dve.tensor_reduce(bad[:, 1:2], neg_rel[:, :], AX_X, ALU.min, negate=True).then_inc(low_ok, 1)
            dve.wait_ge(low_ok, 3)
            dve.tensor_scalar(bad[:, 1:2], bad[:, 1:2], float(1 - P), None, ALU.add).then_inc(setup, 1)
            dve.wait_ge(setup, 8)
            dve.tensor_reduce(bad[:, 3:4], bad[:, 0:3], AX_X, ALU.max).then_inc(setup, 1)
            with dve.Fori(5, tab_rounds) as i:
                table_round(i)
            dve.wait_ge(bad_ok, 1)
            dve.tensor_scalar(flag[:, :], bad_all[:, :], 0.0, None, ALU.is_le).then_inc(flag_ok, 1)
            dve.wait_ge(ix_ld, 16)
            for q in range(2):
                dve.tensor_copy(idx[:, q, :], src_all[:, q * TILES_Q:(q + 1) * TILES_Q]).then_inc(idx_ok, 1)
            dve.wait_ge(flag_ok, 1)
            grouped = dve.value_load(flag[0:1, 0:1], min_val=0, max_val=1)

            def next_sources(q, par, u, i):
                s = 2 * par + u
                dve.wait_ge(kv_ld[s], 16 * TILES_G * (i + 1))
                dve.tensor_copy(idx[:, par, u * TILES_G:(u + 1) * TILES_G],
                                src_all[:, bass.ds((2 * q + u + 4) * TILES_G, TILES_G)])

            def keys_values(q, par, u, i, reuse):
                g = 2 * q + u
                s = 2 * par + u
                dve.wait_ge(kv_ld[s], 16 * TILES_G * (i + 1))
                dve.wait_ge(e_ok, g + 1)
                if reuse:
                    dve.wait_ge(wv_ok, g - 3)
                e4 = e_ps[u][:, :].rearrange("p (t c) -> p t c", c=C).unsqueeze(2)
                dve.tensor_tensor(kve[:, s, :, :, :], kv[:, s, :, :].rearrange("p t (a c) -> p t a c", a=2),
                                  e4.to_broadcast([P, TILES_G, 2, C]), ALU.add).then_inc(kve_ok, 1)

            def products(q, par, u, first_use):
                g = 2 * q + u
                s = 2 * par + u
                dve.wait_ge(q_ok, g + 1)
                dve.wait_ge(kve_ok, g + 1)
                if not (first_use and par == 0):
                    dve.wait_ge(logit_ok, g - 1)
                dve.tensor_tensor(prod[:, u, :].rearrange("p (t c) -> p t c", c=C),
                                  q_ps[u][:, :].rearrange("p (t c) -> p t c", c=C),
                                  kve[:, s, :, 0, :], ALU.mult).then_inc(prod_ok, 1)

            def logits(q, par, u):
                g = 2 * q + u
                dve.wait_ge(prod_ok, g + 1)
                dve.tensor_reduce(logit[:, bass.ds(g * (TILES_G * H), TILES_G * H)],
                                  prod[:, u, :].rearrange("p (h d) -> p h d", d=D), AX_X, ALU.add).then_inc(logit_ok, 1)

            def pair_top(q, first_use=False):
                dve.wait_ge(logit_ok, 2 * q + 2)
                if not first_use:
                    dve.wait_ge(topT_ok, q)
                dve.tensor_reduce(top[:, :], logit[:, bass.ds(q * (TILES_Q * H), TILES_Q * H)], AX_X,
                                  ALU.max).then_inc(top_ok, 1)
                dve.tensor_reduce(lows[:, bass.ds(q, 1)], logit[:, bass.ds(q * (TILES_Q * H), TILES_Q * H)], AX_X,
                                  ALU.min, negate=True).then_inc(lows_ok, 1)

            def pair_max(q, par, first_use=False, between=None):
                dve.wait_ge(topT_ok, q + 1)
                dve.tensor_reduce(neg_pair[:, :], max_ps[0:1, 0:P], AX_X, ALU.max, negate=True).then_inc(negp_ok, 1)
                if between:
                    next_sources(*between)
                dve.wait_ge(negp_ok, q + 1)
                dve.wait_ge(max_ok, q + 1)
                if not first_use:
                    dve.wait_ge(maxb_ok, q)
                dve.tensor_tensor(neg_max[:, par:par + 1], neg_max[:, 1 - par:2 - par], neg_pair[:, :],
                                  ALU.min).then_inc(max_ok, 1)

            def weighted(q, par, u, reuse):
                g = 2 * q + u
                s = 2 * par + u
                dve.wait_ge(exp_ok, q + 1)
                if reuse:
                    dve.wait_ge(sum_ok, g - 3)
                dve.tensor_tensor(wv[:, s, :, 0:C].rearrange("p t (h d) -> p t h d", d=D),
                                  kve[:, s, :, 1, :].rearrange("p t (h d) -> p t h d", d=D),
                                  wv[:, s, :, C:AC].unsqueeze(3).to_broadcast([P, TILES_G, H, D]),
                                  ALU.mult).then_inc(wv_ok, 1)

            def shifts(q, par, u, first_use=False):
                g = 2 * q + u
                if u == 0:
                    dve.wait_ge(fade_ok, q + 1)
                if not first_use:
                    dve.wait_ge(sum_ok, g - 1)
                dve.tensor_scalar(shift[:, u, :], iota_pn[:, :], delta[:, bass.ds(g, 1)],
                                  fade[:, par:par + 1] if u == 0 else one_col[:, :],
                                  ALU.is_equal, ALU.mult).then_inc(shift_ok, 1)

            def step(q, par, i, first_use=False, b_reuse=True, left=ROUND):
                before = not (first_use and par == 0)
                keys_values(q, par, 0, i, not first_use)
                sources = (q, par, 1, i) if left > 0 else None
                if before:
                    pair_max(q - 1, 1 - par, first_use, sources)
                else:
                    next_sources(*sources)
                keys_values(q, par, 1, i, not first_use)
                if before:
                    weighted(q - 1, 1 - par, 0, b_reuse)
                    weighted(q - 1, 1 - par, 1, b_reuse)
                    shifts(q - 1, 1 - par, 0, first_use)
                    shifts(q - 1, 1 - par, 1, first_use)
                for u in range(2):
                    products(q, par, u, first_use)
                for u in range(2):
                    logits(q, par, u)
                if left > 1:
                    next_sources(q + 1, 1 - par, 0, i + par)
                pair_top(q, not before)

            with dve.If(grouped):
                next_sources(0, 0, 0, 0)
                step(0, 0, 0, True, False)
                step(1, 1, 0, True, False)
                step(2, 0, 1, False, False)
                step(3, 1, 1)
                with dve.Fori(1, rounds - 1) as i:
                    for k in range(ROUND):
                        step(ROUND * i + k, k % 2, (ROUND // 2) * i + k // 2)
                for q in range(PAIRS - ROUND, PAIRS):
                    step(q, q % 2, q // 2, left=PAIRS - 2 - q)
                pair_max(PAIRS - 1, 1)
                weighted(PAIRS - 1, 1, 0, True)
                weighted(PAIRS - 1, 1, 1, True)
                shifts(PAIRS - 1, 1, 0)
                shifts(PAIRS - 1, 1, 1)
                dve.wait_ge(lows_ok, PAIRS)
                dve.tensor_reduce(spread[:, 1:2], lows[:, :], AX_X, ALU.max).then_inc(wide_steps, 1)
                dve.wait_ge(negm_ok, PAIRS)
                dve.tensor_scalar(spread[:, 0:1], neg_max_b[:, 1:2], -1.0, None, ALU.mult).then_inc(wide_steps, 1)
            with dve.Else():
                dve.memset(spread[:, 0:2], BIG).then_inc(wide_steps, 2)
            dve.wait_ge(w_ld, 16 * W_DMAS)
            dve.tensor_tensor(w_out[:, :], wbeta[:, 0, :], wbeta[:, 2, :], ALU.add).then_inc(gate_ok, 1)
            dve.tensor_tensor(w_skip[:, :], wbeta[:, 1, :], wbeta[:, 2, :], ALU.subtract).then_inc(gate_ok, 1)
            dve.wait_ge(gate_ok, 2)
            dve.tensor_tensor_reduce(skip_junk[:, :], wskip[:, 0:C], w_skip[:, :], 1.0, 0.0, ALU.mult, ALU.add,
                                     wskip[:, C:C + 1]).then_inc(wskip_ok, 1)
            dve.tensor_copy(skip_row[:, 0:C], bskip[0:1, :])
            dve.wait_ge(wskip_ok, 1)
            dve.tensor_tensor_reduce(skip_junk[0:1, :], bskip[0:1, :], w_skip[0:1, :], 1.0, 0.0, ALU.mult, ALU.add,
                                     skip_row[:, C:C + 1]).then_inc(wskip_ok, 1)

            dve.wait_ge(spread_ok, 1)
            dve.tensor_tensor(spread[:, 0:1], spread[:, 2:3], spread[:, 3:4], ALU.add).then_inc(wide_steps, 1)
            dve.wait_ge(wide_steps, 3)
            dve.tensor_scalar(wide[:, :], spread[:, 0:1], RANGE, 0.0, ALU.is_le, ALU.is_equal).then_inc(wide_ok, 1)
            dve.wait_ge(wide_ok, 1)
            general = dve.value_load(wide[0:1, 0:1], min_val=0, max_val=1)

            def general_tile(t):
                done = [0]

                def link(ins):
                    done[0] += 1
                    ins.then_inc(g_dve, 1)
                    dve.wait_ge(g_dve, G_DVE * t + done[0])

                dve.wait_ge(g_ld, 32 * t + 32)
                for k in range(4):
                    dve.wait_ge(g_get[k], 16 * t + 16)
                dve.wait_ge(g_pe, 3 * t + 1)
                link(dve.tensor_tensor(g_kve, g_kv.rearrange("p (a c) -> p a c", a=2),
                                       e_ps[0][:, 0:C].unsqueeze(1).to_broadcast([P, 2, C]), ALU.add))
                link(dve.tensor_tensor(g_prod, g_kve[:, 0, :], g_q, ALU.mult))
                link(dve.tensor_reduce(g_logit[:, :], g_prod.rearrange("p (h d) -> p h d", d=D), AX_X, ALU.add))
                link(dve.tensor_copy(g_own, g_logit[:, :].unsqueeze(2).to_broadcast([P, H, P])))
                assert done[0] == G_OWN
                link(dve.tensor_copy(g_dst_f, g_dst))
                link(dve.tensor_copy(g_node[:, 0:1], dst_all[:, bass.ds(t, 1)]))
                link(dve.tensor_scalar(g_same, g_dst_f, g_node[:, 0:1], None, ALU.is_equal))
                link(dve.tensor_scalar(g_apart, g_same, -1.0, BIG, ALU.add, ALU.mult))
                link(dve.scalar_tensor_tensor(g_before, iota_pn[:, :], 0.0, g_same, ALU.is_gt, ALU.mult))
                link(dve.tensor_reduce(g_node[:, 1:2], g_before, AX_X, ALU.max))
                link(dve.tensor_scalar(g_put[:, :], g_node[:, 1:2], float(ROWS), g_node[:, 0:1], ALU.mult, ALU.add))
                dve.wait_ge(g_pe, 3 * t + 2)
                link(dve.tensor_tensor(g_peers[:, 0:4, :], q_ps[0][:, :].rearrange("p (h e) -> p h e", e=P),
                                       g_same.unsqueeze(1).to_broadcast([P, 4, P]), ALU.mult))
                link(dve.tensor_tensor(g_peers[:, 4:H, :], q_ps[1][:, :].rearrange("p (h e) -> p h e", e=P),
                                       g_same.unsqueeze(1).to_broadcast([P, 4, P]), ALU.mult))
                link(dve.tensor_tensor(g_peers, g_peers, g_apart.unsqueeze(1).to_broadcast([P, H, P]), ALU.add))
                link(dve.tensor_reduce(g_max[:, :], g_peers, AX_X, ALU.max))
                link(dve.tensor_tensor(g_max[:, :], g_max[:, :], g_old_max[:, :], ALU.max))
                link(dve.tensor_tensor(g_exp[:, 0, :], g_logit[:, :], g_max[:, :], ALU.subtract))
                link(dve.tensor_tensor(g_exp[:, 1, :], g_old_max[:, :], g_max[:, :], ALU.subtract))
                assert done[0] == G_EXP
                dve.wait_ge(g_act, t + 1)
                link(dve.tensor_copy(g_wv[:, C:AC], g_exp[:, 0, :]))
                link(dve.tensor_tensor(g_wv[:, 0:C].rearrange("p (h d) -> p h d", d=D),
                                       g_kve[:, 1, :].rearrange("p (h d) -> p h d", d=D),
                                       g_exp[:, 0, :].unsqueeze(2).to_broadcast([P, H, D]), ALU.mult))
                assert done[0] == G_WV
                link(dve.tensor_tensor(g_old[:, 0:C].rearrange("p (h d) -> p h d", d=D),
                                       g_old[:, 0:C].rearrange("p (h d) -> p h d", d=D),
                                       g_exp[:, 1, :].unsqueeze(2).to_broadcast([P, H, D]), ALU.mult))
                link(dve.tensor_tensor(g_old[:, C:AC], g_old[:, C:AC], g_exp[:, 1, :], ALU.mult))
                dve.wait_ge(g_pe, 3 * t + 3)
                link(dve.tensor_tensor(g_new, sum_ps[0][:, 0:AC], g_old, ALU.add))
                assert done[0] == G_DVE

            with dve.If(general):
                dve.memset(g_low, -BIG).then_inc(g_low_ok, 1)
                with dve.Fori(0, TILES) as t:
                    general_tile(t)

            def heads(ap):
                return ap.rearrange("p b (h d) -> p b h d", d=D)

            def attention(b, p, i):
                dve.wait_ge(n_ld[p], 16 * (i + 1))
                dve.tensor_scalar(n_rz[:, p, :, :], n_sum[p][:, :, C:AC], 1e-30, None, ALU.max).then_inc(z_ok, 1)
                dve.wait_ge(z_ok, b + 1)
                dve.reciprocal(n_rz[:, p, :, :], n_rz[:, p, :, :]).then_inc(rz_ok, 1)
                dve.wait_ge(rz_ok, b + 1)
                dve.tensor_tensor(heads(n_att[p]), heads(n_sum[p][:, :, 0:C]),
                                  n_rz[:, p, :, :].unsqueeze(3).to_broadcast([P, FB, H, D]), ALU.mult
                                  ).then_inc(att_ok, 1)

            def gate_score(b, p):
                dve.wait_ge(att_ok, b + 1)
                for k in range(FB):
                    last = dve.tensor_tensor_reduce(n_junk[:, k, :], n_att[p][:, k, :], w_out[:, :], 1.0, 0.0, ALU.mult,
                                                    ALU.add, n_gate[:, p, 0, k:k + 1])
                last.then_inc(score_ok, 1)
                dve.wait_ge(skip_ok, b + 1)
                dve.wait_ge(score_ok, b + 1)
                dve.tensor_tensor(n_gate[:, p, 1, :], n_gate[:, p, 0, :], n_skip[p][:, :, C], ALU.add
                                  ).then_inc(total_ok, 1)

            def mix(b, p):
                dve.wait_ge(gexp_ok, b + 1)
                dve.tensor_scalar(n_gate[:, p, 2, :], n_gate[:, p, 2, :], 1.0, None, ALU.add).then_inc(gden_ok, 1)
                dve.wait_ge(gden_ok, b + 1)
                dve.reciprocal(n_gate[:, p, 2, :], n_gate[:, p, 2, :]).then_inc(gate_done, 1)
                dve.wait_ge(diff_ok, b + 1)
                dve.wait_ge(gate_done, b + 1)
                for k in range(FB):
                    last = dve.scalar_tensor_tensor(n_att[p][:, k, :], n_skip[p][:, k, 0:C], n_gate[:, p, 2, k:k + 1],
                                                    n_att[p][:, k, :], ALU.mult, ALU.add)
                last.then_inc(mix_ok, 1)
                dve.wait_ge(mix_ok, b + 1)
                statistics(b, p, 0, n_att)

            def statistics(b, p, k, rows):
                for j in range(FB):
                    last = dve.bn_stats(n_bn[:, k, j, :], rows[p][:, j, :])
                last.then_inc(bn_ok[k], 1)
                dve.wait_ge(bn_ok[k], b + 1)
                dve.sem_inc(stats_in, 1)
                for j in range(FB):
                    last = dve.bn_aggr(n_mv[:, p, k, j, :], n_bn[:, k, j, :])
                last.then_inc(mv_ok[k], 1)

            def offsets(b, p, k):
                dve.wait_ge(mv_ok[k], b + 1)
                dve.wait_ge(inv_ok[k], b + 1)
                dve.scalar_tensor_tensor(n_off[:, p, k, :], n_mv[:, p, k, :, 0], -1.0, n_inv[:, p, k, :],
                                         ALU.mult, ALU.mult).then_inc(off_ok[k], 1)

            def residual(b, p, reuse, i):
                dve.wait_ge(twice_ok, b + 1)
                dve.wait_ge(beta_ok, b + 1)
                if reuse:
                    dve.wait_ge(n_out[p], 16 * i)
                dve.scalar_tensor_tensor(n_res[p], n_att[p], 0.0, n_x[p], ALU.max, ALU.add).then_inc(res_ok, 1)

            def second_statistics(b, p):
                dve.wait_ge(res_ok, b + 1)
                statistics(b, p, 1, n_res)

            def node_step(b, p, i, reuse=True, before=2, after=True):
                mix(b, p)
                if before == 2:
                    offsets(b - 2, p, 1)
                if before:
                    residual(b - 1, 1 - p, reuse, i + p - 1)
                if after:
                    attention(b + 1, 1 - p, i + p)
                offsets(b, p, 0)
                if after:
                    gate_score(b + 1, 1 - p)
                if before:
                    second_statistics(b - 1, 1 - p)

            attention(0, 0, 0)
            gate_score(0, 0)
            node_step(0, 0, 0, before=0)
            node_step(1, 1, 0, reuse=False, before=1)
            node_step(2, 0, 1, reuse=False)
            node_step(3, 1, 1)
            with dve.Fori(2, batches // 2 - 1) as i:
                node_step(2 * i, 0, i)
                node_step(2 * i + 1, 1, i)
            node_step(batches - 2, 0, batches // 2 - 1)
            node_step(batches - 1, 1, batches // 2 - 1, after=False)
            offsets(batches - 2, 0, 1)
            residual(batches - 1, 1, True, batches // 2 - 1)
            second_statistics(batches - 1, 1)
            offsets(batches - 1, 1, 1)


_WEIGHTS = ("Wq", "bq", "Wk", "bk", "Wv", "bv", "We", "Wskip", "bskip", "Wbeta", "ln_gamma", "ln_beta")


def kernel(**inputs):
    import numpy as np
    import concourse.bacc as bacc
    from concourse.bass_utils import run_bass_kernel_spmd

    x = np.zeros((ROWS, C), np.float32)
    x[:N_NODES] = inputs["x"]
    ea = np.zeros((C, EDGES), np.float32)
    ea[:, :N_EDGES] = np.asarray(inputs["edge_attr_128"]).T
    src = np.zeros(EDGES, np.int32)
    src[:N_EDGES] = inputs["src"]
    dst = np.full(EDGES, N_NODES, np.int32)
    dst[:N_EDGES] = inputs["dst"]
    arrays = {
        "x": x, "xT": np.ascontiguousarray(x.T), "eaT": ea,
        "srcT": np.ascontiguousarray(src.reshape(TILES, P).T),
        "dstT": np.ascontiguousarray(dst.reshape(TILES, P).T),
        "dst": dst,
    }
    for name in _WEIGHTS:
        a = np.ascontiguousarray(inputs["L0_gnn_" + name])
        arrays["w_" + name] = a.reshape(-1) if name == "Wbeta" else a

    nc = bacc.Bacc("TRN2", target_bir_lowering=False, num_devices=1)
    aps = {n: nc.dram_tensor(n, a.shape, mybir.dt.from_np(a.dtype), kind="ExternalInput").ap()
           for n, a in arrays.items()}
    out = nc.dram_tensor("out", (OUT_BLOCKS * P, C), F32, kind="ExternalOutput").ap()
    build(nc, aps["xT"], aps["x"], aps["eaT"], aps["srcT"], aps["dstT"], aps["dst"],
          {n: aps["w_" + n] for n in _WEIGHTS}, out)
    r = run_bass_kernel_spmd(nc, [arrays], core_ids=[0])
    return r.results[0]["out"][:N_NODES]
```
